# Optimizing a Trainium2 kernel written in Bass

```python
import numpy as np
import jax
import jax.numpy as jnp

def _softmax(x, axis=-1):
    return jax.nn.softmax(x, axis=axis)

def _gelu(x):
    return jax.nn.gelu(x, approximate=True)

def _silu(x):
    return jax.nn.silu(x)

def _sigmoid(x):
    return jax.nn.sigmoid(x)

def _layernorm(x, axis=-1, eps=1e-05):
    m = jnp.mean(x, axis=axis, keepdims=True)
    v = jnp.var(x, axis=axis, keepdims=True)
    return (x - m) / jnp.sqrt(v + eps)

def _scatter_add(tgt, idx, src, axis=0):
    return tgt.at[idx].add(src)

def _segment_sum(src, seg, n):
    return jax.ops.segment_sum(src, seg, n)
kernel_name = 'mk_early_fusion_d1_tok_img768_r4_543e65'

def setup_inputs(seed: int=0):
    np.random.seed(seed)
    _w = jnp.asarray

    def _rec_inputs():
        import jax
        import jax.numpy as jnp
        _rk = jax.random.key(seed)
        x = 7.57192e-06 + 1.00007 * jax.random.normal(jax.random.fold_in(_rk, 1), (32, 3, 224, 224), jnp.float32)
        txt = 0.00277252 + 1.14258 * jax.random.normal(jax.random.fold_in(_rk, 2), (32, 77, 192), jnp.float32)
        return (x, txt)
    x, txt = _rec_inputs()

    def _L0_tok_setup():
        import jax, jax.numpy as jnp
        import numpy as np
        from jax import lax
        P = 16
        S = 8
        key = jax.random.key(seed)
        k1, k2, k3, k4, k5 = jax.random.split(key, 5)
        B, C, H, W = (64, 3, 224, 224)
        D = 192
        patch_dim = C * P * P
        out = (H - P) // S + 1
        n_tok = out * out + 1
        return {'x': jax.random.normal(k1, (B, C, H, W), dtype=jnp.float32), 'w': jax.random.normal(k2, (D, patch_dim), dtype=jnp.float32) * 0.02, 'b': jax.random.normal(k3, (D,), dtype=jnp.float32) * 0.02, 'cls_token': jax.random.normal(k4, (1, 1, D), dtype=jnp.float32), 'pos_embedding': jax.random.normal(k5, (1, n_tok, D), dtype=jnp.float32)}
    _L0_tok_all = _L0_tok_setup()
    _L0_tok_in = {k: v for k, v in _L0_tok_all.items() if k in ('w', 'b', 'cls_token', 'pos_embedding')}
    del _L0_tok_all

    def _L0_attn_setup():
        import jax, jax.numpy as jnp
        import numpy as np
        import math
        DIM = 192
        NUM_HEADS = 12

        def _xavier_uniform(key, out_f, in_f):
            a = math.sqrt(6.0 / (in_f + out_f))
            return jax.random.uniform(key, (out_f, in_f), jnp.float32, -a, a)
        key = jax.random.key(seed)
        k_x, k_qw, k_qB, k_pw, k_pB = jax.random.split(key, 5)
        B, N = (16, 256)
        x = jax.random.normal(k_x, (B, N, DIM), jnp.float32)
        qkv_w = _xavier_uniform(k_qw, 3 * DIM, DIM)
        qkv_b = jnp.zeros((3 * DIM,), jnp.float32)
        qkv_B = jax.random.normal(k_qB, (3 * DIM, DIM), jnp.float32) * math.sqrt(1.0 / DIM)
        proj_w = _xavier_uniform(k_pw, DIM, DIM)
        proj_b = jnp.zeros((DIM,), jnp.float32)
        proj_B = jax.random.normal(k_pB, (DIM, DIM), jnp.float32) * math.sqrt(1.0 / DIM)
        return {'x': x, 'qkv_w': qkv_w, 'qkv_b': qkv_b, 'qkv_B': qkv_B, 'proj_w': proj_w, 'proj_b': proj_b, 'proj_B': proj_B}
    _L0_attn_all = _L0_attn_setup()
    _L0_attn_in = {k: v for k, v in _L0_attn_all.items() if k in ('qkv_w', 'qkv_b', 'qkv_B', 'proj_w', 'proj_b', 'proj_B')}
    del _L0_attn_all

    def _L0_ffn_setup():
        import jax, jax.numpy as jnp
        import numpy as np
        EPS = 1e-06

        def l2_normalize(x, axis):
            norm = jnp.sqrt(jnp.square(x).sum(axis=axis, keepdims=True))
            return x * (1.0 / (norm + EPS))
        key = jax.random.key(seed)
        ks = jax.random.split(key, 8)
        b, m, d = (32, 256, 192)
        n, p = (8, 4)
        h = d // 8
        X = jax.random.normal(ks[0], (b, m, d), dtype=jnp.float32)
        std_slot = float(np.sqrt(2.0 / (d + n * p)))
        slot_params = jax.random.normal(ks[1], (d, n, p), dtype=jnp.float32) * std_slot
        scale = jnp.ones((), dtype=jnp.float32)
        W_down = jax.random.normal(ks[2], (n, d, h), dtype=jnp.float32) * float(np.sqrt(1.0 / d))
        b_down = jnp.zeros((n, h), dtype=jnp.float32)
        W_up = jax.random.normal(ks[3], (n, h, d), dtype=jnp.float32) * float(np.sqrt(1.0 / h))
        b_up = jnp.zeros((n, d), dtype=jnp.float32)
        return {'X': X, 'slot_params': slot_params, 'scale': scale, 'W_down': W_down, 'b_down': b_down, 'W_up': W_up, 'b_up': b_up}
    _L0_ffn_all = _L0_ffn_setup()
    _L0_ffn_in = {k: v for k, v in _L0_ffn_all.items() if k in ('slot_params', 'scale', 'W_down', 'b_down', 'W_up', 'b_up')}
    del _L0_ffn_all
    return {'x': x, 'txt': txt, 'L0_tok_w': _L0_tok_in['w'], 'L0_tok_b': _L0_tok_in['b'], 'L0_tok_cls_token': _L0_tok_in['cls_token'], 'L0_tok_pos_embedding': _L0_tok_in['pos_embedding'], 'L0_attn_qkv_w': _L0_attn_in['qkv_w'], 'L0_attn_qkv_b': _L0_attn_in['qkv_b'], 'L0_attn_qkv_B': _L0_attn_in['qkv_B'], 'L0_attn_proj_w': _L0_attn_in['proj_w'], 'L0_attn_proj_b': _L0_attn_in['proj_b'], 'L0_attn_proj_B': _L0_attn_in['proj_B'], 'L0_ffn_slot_params': _L0_ffn_in['slot_params'], 'L0_ffn_scale': _L0_ffn_in['scale'], 'L0_ffn_W_down': _L0_ffn_in['W_down'], 'L0_ffn_b_down': _L0_ffn_in['b_down'], 'L0_ffn_W_up': _L0_ffn_in['W_up'], 'L0_ffn_b_up': _L0_ffn_in['b_up']}

def reference(x, txt, L0_tok_w, L0_tok_b, L0_tok_cls_token, L0_tok_pos_embedding, L0_attn_qkv_w, L0_attn_qkv_b, L0_attn_qkv_B, L0_attn_proj_w, L0_attn_proj_b, L0_attn_proj_B, L0_ffn_slot_params, L0_ffn_scale, L0_ffn_W_down, L0_ffn_b_down, L0_ffn_W_up, L0_ffn_b_up):
    import jax
    import jax.numpy as jnp

    def _L0_tok_ref(x, w, b, cls_token, pos_embedding):
        import jax, jax.numpy as jnp
        import numpy as np
        from jax import lax
        P = 16
        S = 8
        B = x.shape[0]
        patches = lax.conv_general_dilated_patches(x, filter_shape=(P, P), window_strides=(S, S), padding='VALID', dimension_numbers=('NCHW', 'OIHW', 'NCHW'))
        pd = patches.shape[1]
        patches = patches.reshape(B, pd, -1).transpose(0, 2, 1)
        tok = jnp.einsum('bnp,dp->bnd', patches, w) + b
        cls = jnp.broadcast_to(cls_token, (B, 1, tok.shape[-1]))
        out = jnp.concatenate([cls, tok], axis=1) + pos_embedding
        return out

    def _L0_attn_ref(x, qkv_w, qkv_b, qkv_B, proj_w, proj_b, proj_B):
        import jax, jax.numpy as jnp
        import numpy as np
        import math
        DIM = 192
        NUM_HEADS = 12

        def _xavier_uniform(key, out_f, in_f):
            a = math.sqrt(6.0 / (in_f + out_f))
            return jax.random.uniform(key, (out_f, in_f), jnp.float32, -a, a)
        B, N, C = x.shape
        hd = C // NUM_HEADS
        scale = hd ** (-0.5)
        qkv = x @ qkv_w.T + qkv_b
        qkv = qkv.reshape(B, N, 3, NUM_HEADS, hd).transpose(2, 0, 3, 1, 4)
        q, k, v = (qkv[0], qkv[1], qkv[2])
        attn = jnp.einsum('bhnd,bhmd->bhnm', q, k) * scale
        attn = jax.nn.softmax(attn, axis=-1)
        out = jnp.einsum('bhnm,bhmd->bhnd', attn, v)
        out = out.transpose(0, 2, 1, 3).reshape(B, N, C)
        return out @ proj_w.T + proj_b

    def _L0_ffn_ref(X, slot_params, scale, W_down, b_down, W_up, b_up):
        import jax, jax.numpy as jnp
        import numpy as np
        EPS = 1e-06

        def l2_normalize(x, axis):
            norm = jnp.sqrt(jnp.square(x).sum(axis=axis, keepdims=True))
            return x * (1.0 / (norm + EPS))
        b, m, d = X.shape
        _, n, p = slot_params.shape
        Xn = l2_normalize(X, axis=-1)
        sp = l2_normalize(slot_params, axis=1) * scale
        logits = jnp.einsum('bmd,dnp->bmnp', Xn, sp)
        D = jax.nn.softmax(logits, axis=1)
        C = jax.nn.softmax(logits.reshape(b, m, n * p), axis=2).reshape(b, m, n, p)
        X_tilde = jnp.einsum('bmd,bmnp->bnpd', Xn, D)
        H = jax.nn.gelu(jnp.einsum('bnpd,ndh->bnph', X_tilde, W_down) + b_down[None, :, None, :], approximate=False)
        Y_tilde = jnp.einsum('bnph,nhd->bnpd', H, W_up) + b_up[None, :, None, :]
        Y = jnp.einsum('bnpd,bmnp->bmd', Y_tilde, C)
        return Y
    h = _L0_tok_ref(x, L0_tok_w, L0_tok_b, L0_tok_cls_token, L0_tok_pos_embedding)
    h = jnp.concatenate([h, txt], axis=1)
    h = h + _L0_attn_ref(_layernorm(h, axis=-1), L0_attn_qkv_w, L0_attn_qkv_b, L0_attn_qkv_B, L0_attn_proj_w, L0_attn_proj_b, L0_attn_proj_B)
    h = h + _L0_ffn_ref(_layernorm(h, axis=-1), L0_ffn_slot_params, L0_ffn_scale, L0_ffn_W_down, L0_ffn_b_down, L0_ffn_W_up, L0_ffn_b_up)
    return h

_drawn_inputs = setup_inputs


def setup_inputs(seed=0):
    import zlib

    import numpy as np

    out = dict(_drawn_inputs(seed))
    spreads = {'L0_attn_qkv_b': (0.0, 0.1),
     'L0_attn_proj_b': (0.0, 0.1),
     'L0_ffn_b_down': (0.0, 0.478),
     'L0_ffn_b_up': (0.0, 0.1)}
    factors = {'L0_tok_b': 2.96, 'L0_ffn_slot_params': 8.0, 'L0_ffn_W_down': 8.0, 'L0_ffn_W_up': 3.389}
    for name, (base, spread) in spreads.items():
        noise = np.random.default_rng([zlib.crc32(name.encode()), seed]).standard_normal(out[name].shape)
        drawn = base * np.exp(spread * noise) if base else spread * noise
        out[name] = jnp.asarray(drawn.astype(out[name].dtype))
    for name, factor in factors.items():
        out[name] = (out[name] * factor).astype(out[name].dtype)
    return out
```

```python
from contextlib import ExitStack

import concourse.bass as bass
from concourse import mybir

ALU = mybir.AluOpType
ACT = mybir.ActivationFunctionType
AX = mybir.AxisListType
F32 = mybir.dt.float32
BF16 = mybir.dt.bfloat16

C, IMG, P, S, D = 3, 224, 16, 8, 192
G = (IMG - P) // S + 1
BG = IMG // S
TXT = 77
NH, HD = 12, 16
NEXP, SLOTS, HID = 8, 4, 24
NS = NEXP * SLOTS
N = G * G + 1 + TXT
NT = 7
GR = 4
TG = GR * G
TGL = G * G - (NT - 1) * TG
TX = 7
TS = TG + TX
TL = N - (NT - 1) * TS
NP = N + 1
HF = NP // 2
KB = 6
KR = KB * HD
KS = KR + 2
NG = NH // 4
UNITS = NG * NT
TILES = UNITS * 4
Q_PARTS = (0, 0, 1, 1, 0, 2)
K_PARTS = (0, 1, 0, 1, 2, 0)
LN_EPS, L2_EPS = 1e-5, 1e-6
LIMIT = 36.0
ERF_NUM = (0.00022905065861350646, 0.0034082910107109506, 0.050955695062380861, 0.18520832239976145,
           1.128379143519084)
ERF_DEN = (-1.1791602954361697e-7, 0.000023547966471313185, 0.0010179625278914885, 0.014070470171167667,
           0.11098505178285362, 0.49746925110067538, 1.0)
ERF_MAX = 3.7439211627767994

PER = dict(
    x_loaded=48, txt_loaded=32, a_filled=21, a_drained=21, a_chain=2, bound_chain=3, flag_ready=1, flag_seen=3, ln1_pool=2, xn_ready=1,
    hi_ready=8, r_ready=8, mid_ready=4, parts_ready=4, parts_written_0=32, parts_written_1=32,
    group_loaded_0=192, group_loaded_1=192, group_loaded_2=192, m_loaded=384, shift_written=16,
    shift_loaded_0=16, shift_loaded_1=16, shift_loaded_2=16, s_filled=84, exp_done=84, pv_done=21, o_bcast=3, o_guess=6, o_chain=6, o_ready=3,
    m_filled=86, m_drained=84, m_chain=2, shift_ready=1,
    c_filled=21, c_drained=21, c_chain=25, ln2_pool=8, x2_ready=1, disp_exp=1, comb_exp=1, diag_ready=1,
    hidden_ready=1, out_written=80,
)


def early_fusion(nc, B, t, scr_parts, scr_shift, out):
    with ExitStack() as ctx:
        def sb(name, shape, dt=F32):
            return ctx.enter_context(nc.sbuf_tensor(name, shape, dt))

        sem = {name: ctx.enter_context(nc.semaphore(name)) for name in PER}
        params_loaded = ctx.enter_context(nc.semaphore("params_loaded"))
        cls_placed = ctx.enter_context(nc.semaphore("cls_placed"))
        setup_dve = ctx.enter_context(nc.semaphore("setup_dve"))
        setup_pool = ctx.enter_context(nc.semaphore("setup_pool"))
        setup_done = ctx.enter_context(nc.semaphore("setup_done"))

        w_conv = sb("w_conv_sb", [128, 6, D])
        w_qk = sb("w_qk_sb", [96, 2, 4 * 96])
        b_qk = sb("b_qk_sb", [96, 4])
        w_v = sb("w_v_sb", [97, 2, D])
        w_p = sb("w_p_sb", [128, NG, D])
        pos = sb("pos_sb", [TG, NT, D])
        slots = sb("slots_sb", [96, 2, NS])
        w_down = sb("w_down_sb", [96, 2, D])
        b_down = sb("b_down_sb", [96, 2])
        w_up = sb("w_up_sb", [96, 2, D])
        b_up = sb("b_up_sb", [NS, D])
        ident = sb("ident_sb", [128, 128])
        mask = sb("mask_sb", [96, 2, NS])
        cls = sb("cls_sb", [1, 2, D])
        tokb = sb("tokb_sb", [TG, D])
        scale_c = sb("scale_c", [96, 1])
        sq = sb("sq", [96, 2, NS])
        nrm = sb("nrm", [96, 2, SLOTS])
        const = sb("const", [128, 7, 8])
        held = sb("held", [1, 8])

        xa = sb("xa_sb", [128, 2, BG * G])
        xb = sb("xb_sb", [128, BG * G])
        h = sb("h", [TL, 2, NT, D])
        xn = sb("xn", [TL, NT, D])
        xnT = sb("xnT", [97, 2, NP])
        st = sb("st", [TL, NT, 6])
        mv = sb("mv", [TL, NT, 2])
        ve = sb("ve", [TL, 8])
        rstd = sb("rstd", [TL, 8])
        f = sb("f", [96, 2, NP])
        r = sb("r", [96, 2, NP])
        parts = sb("parts", [96, 2, 3, NP], BF16)
        Qs = sb("Qs", [KS, 2, 4, NP], BF16)
        Ks = sb("Ks", [KS, 2, 4, NP], BF16)
        v = sb("v", [TL, 2, NT, NH, HD + 1])
        top = sb("top", [96, 4, 2])
        bound = sb("bound", [96, 2])
        most = sb("most", [1, 1])
        flag = sb("flag", [1, 2], mybir.dt.int32)
        head_rows = sb("head_rows_sb", [96, 6])
        mx = sb("mx", [TL, NT, NH])
        neg = sb("neg", [NH, NP])
        shift = sb("shift", [NH, 2, NP], BF16)
        probs = sb("probs", [TL, 2, 4, NP])
        den = sb("den", [128, NP])
        rec = sb("rec", [128, NP])
        oT = sb("oT", [128, NG, NP])
        h2 = sb("h2", [TL, NT, D])
        x2 = sb("x2", [TL, NT, D])
        x2T = sb("x2T", [96, 2, NP])
        st2 = sb("st2", [TL, NT, 6])
        mv2 = sb("mv2", [TL, NT, 2])
        ve2 = sb("ve2", [TL, 8])
        rstd2 = sb("rstd2", [TL, 8])
        nr2 = sb("nr2", [TL, 8])
        sc2 = sb("sc2", [TL, 8])
        lT = sb("lT", [NS, NP])
        nmax = sb("nmax", [NS, 1])
        dsum = sb("dsum", [NS, 1])
        drec = sb("drec", [NS, 1])
        diag = sb("diag", [NS, NS])
        lc = sb("lc", [TL, NT, NS])
        cmax = sb("cmax", [TL, NT])
        csum = sb("csum", [TL, NT])
        crec = sb("crec", [TL, NT])
        disp = sb("disp", [TL, NT, NS])
        cT = sb("cT", [NS, NP])
        xt = sb("xt", [96, 2, NS])
        u = sb("u", [96, 2, NS])
        uc = sb("uc", [96, 2, NS])
        u2 = sb("u2", [96, 2, NS])
        pn = sb("pn", [96, 2, NS])
        pd = sb("pd", [96, 2, NS])
        hm = sb("hm", [96, 2, NS])
        yt = sb("yt", [NS, D])
        y = sb("y", [TL, NT, D])

        ps_s = ctx.enter_context(nc.psum_tensor("ps_s", [128, 2, 2, 512], F32))
        ps_o = ctx.enter_context(nc.psum_tensor("ps_o", [128, 2, 512], F32))
        ps_a = ctx.enter_context(nc.psum_tensor("ps_a", [128, 512], F32))
        ps_c = ctx.enter_context(nc.psum_tensor("ps_c", [128, 512], F32))

        def upto(name, image, count):
            value = image * PER[name] + count
            return max(value, 0) if isinstance(value, int) else value

        def rows(tile):
            return TL if tile == NT - 1 else TS

        a_slot = [0, 1, 2, 3] + [5, 6, 7, 8] + list(range(9, 17)) + [17, 17, 18, 19, 20]
        a_at = {slot: [k for k, at in enumerate(a_slot) if at == slot] for slot in range(UNITS)}
        v_fill = {16: 0, 18: 1, 19: 2, 20: 3}
        c_slot = [0, 1, 2, 3] + [5, 6, 7, 8] + [9, 10, 10, 12, 12, 13, 14, 15, 16] + [17, 18, 19, 20]
        c_at = {slot: [k for k, at in enumerate(c_slot) if at == slot] for slot in range(UNITS)}
        pairs = [(0, 1), (2, 3), (4, 5), (6,)]
        quads = [(half, ts) for half in range(2) for ts in ((0, 1, 2, 3), (4, 5, 6))]

        block = ctx.enter_context(nc.Block())

        @block.sync
        def _(sp):
            load = lambda dst, src: sp.dma_start(dst, src).then_inc(params_loaded, 16)
            load(w_conv[:], t["w_conv"])
            load(w_qk[:], t["w_qk"])
            load(b_qk[:], t["b_qk"])
            load(w_v[:], t["w_v"])
            load(pos[:], t["pos"])
            load(tokb[:], t["tok_b"].partition_broadcast(TG))
            load(cls[:, :, :], t["cls"])
            load(ident[:], t["ident"])
            load(w_p[:], t["w_p"])
            load(slots[:], t["slots"])
            load(scale_c[:], t["slot_scale"].partition_broadcast(96))
            load(w_down[:], t["w_down"])
            load(b_down[:], t["b_down"])
            load(w_up[:], t["w_up"])
            load(b_up[:], t["b_up"])
            load(mask[:], t["expert_mask"])
            load(head_rows[:], t["head_rows"])

            def load_x(a):
                sp.wait_ge(sem["a_filled"], upto("a_filled", a - 1, 4))
                src = t["x"][bass.ds(a, 1)].rearrange("a s p n -> p (a s) n")
                sp.dma_start(xa[:], src[0:128]).then_inc(sem["x_loaded"], 16)
                sp.dma_start(xb[0:64], src[128:192, 0]).then_inc(sem["x_loaded"], 16)
                sp.dma_start(xb[64:128], src[128:192, 1]).then_inc(sem["x_loaded"], 16)

            def load_txt(a, half):
                if not isinstance(a, int) or a >= 2:
                    sp.wait_ge(sem["c_drained"], upto("c_drained", a - 2, 4))
                src = t["txt"][bass.ds(a, 1)].rearrange("a n d -> (a n) d")
                sp.dma_start(h[TG:TS, half, 0:NT - 1, :],
                             src[0:TX * (NT - 1)].rearrange("(t r) d -> r t d", r=TX)).then_inc(sem["txt_loaded"], 16)
                sp.dma_start(h[TGL + 1:TL, half, NT - 1, :], src[TX * (NT - 1):]).then_inc(sem["txt_loaded"], 16)

            def write_parts(a):
                for c in range(4):
                    if c == 0:
                        sp.wait_ge(sem["group_loaded_2"], upto("group_loaded_2", a, 0))
                    sp.wait_ge(sem["parts_ready"], upto("parts_ready", a, c + 1))
                    sp.dma_start(scr_parts[c], parts[:, c % 2])\
                        .then_inc(sem[f"parts_written_{c % 2}"], 16)

            def load_group(g, half, signal):
                for first, dst, which in ((0, Qs, Q_PARTS), (2, Ks, K_PARTS)):
                    src = scr_parts[first:first + 2].rearrange("c (h d) s n -> d (c h) s n", d=HD)
                    for b, part in enumerate(which):
                        sp.dma_start(dst[HD * b:HD * b + HD, half], src[:, 4 * g:4 * g + 4, part])\
                            .then_inc(sem[signal], 16)

            def load_shift(g, half):
                sp.dma_start(Qs[KR:KS, half], scr_shift[:, 4 * g:4 * g + 4])\
                    .then_inc(sem[f"shift_loaded_{g}"], 16)

            def load_for_maxima(a, half):
                for g in (1, 2):
                    if g == 1:
                        sp.wait_ge(sem["s_filled"], upto("s_filled", a, 0))
                    else:
                        sp.wait_ge(sem["m_filled"], upto("m_filled", a, 56))
                    load_group(g, half, "m_loaded")

            def send_shift(a, half):
                sp.wait_ge(sem["shift_ready"], upto("shift_ready", a, 1))
                sp.dma_start(scr_shift.rearrange("s h n -> h s n"), shift[:]).then_inc(sem["shift_written"], 16)
                sp.wait_ge(sem["shift_written"], upto("shift_written", a, 16))
                load_shift(0, half)

            def store(c):
                dst = out[bass.ds(c, 1)].rearrange("a n d -> (a n) d")
                sp.wait_ge(sem["c_drained"], upto("c_drained", c, 21))
                put = lambda d, s: sp.dma_start(d, s).then_inc(sem["out_written"], 16)
                put(dst[1:1 + TG * (NT - 1)].rearrange("(t p) d -> p t d", p=TG), y[0:TG, 0:NT - 1])
                put(dst[1 + TG * (NT - 1):1 + G * G], y[0:TGL, NT - 1])
                put(dst[0:1], y[TGL:TGL + 1, NT - 1])
                put(dst[1 + G * G:1 + G * G + TX * (NT - 1)].rearrange("(t r) d -> r t d", r=TX), y[TG:TS, 0:NT - 1])
                put(dst[1 + G * G + TX * (NT - 1):N], y[TGL + 1:TL, NT - 1])

            load_x(0)
            sp.wait_ge(setup_done, 1)
            for half in range(2):
                sp.dma_start(h[TGL:TGL + 1, half, NT - 1, :], cls[0:1, 0, :]).then_inc(cls_placed, 16)

            def step(i, prep, att, fin, parity, ahead=True):
                if att:
                    sp.wait_ge(sem["s_filled"], upto("s_filled", i, 0))
                    sp.wait_ge(sem["m_filled"], upto("m_filled", i, 84))
                    sp.wait_ge(sem["shift_written"], upto("shift_written", i, 16))
                    load_group(1, 1 - parity, "group_loaded_1")
                    load_shift(1, 1 - parity)
                if prep:
                    load_txt(i + 1, 1 - parity)
                    if ahead:
                        load_x(i + 2)
                if att:
                    sp.wait_ge(sem["s_filled"], upto("s_filled", i, 28))
                    load_group(2, parity, "group_loaded_2")
                    load_shift(2, parity)
                if prep:
                    write_parts(i + 1)
                    sp.wait_ge(sem["s_filled"], upto("s_filled", i, 56))
                    for c in range(2):
                        sp.wait_ge(sem[f"parts_written_{c}"], upto(f"parts_written_{c}", i + 1, 32))
                    load_group(0, 1 - parity, "group_loaded_0")
                if prep:
                    sp.wait_ge(sem["flag_ready"], upto("flag_ready", i + 1, 1))
                    sp.sem_inc(sem["flag_seen"], 1)
                    with sp.If(sp.value_load(flag[0:1, 1 - parity:2 - parity]) > 0):
                        load_for_maxima(i + 1, parity)
                        send_shift(i + 1, 1 - parity)
                    with sp.Else():
                        sp.sem_inc(sem["m_loaded"], PER["m_loaded"])
                        sp.dma_start(scr_shift, t["no_shift"]).then_inc(sem["shift_written"], 16)
                        sp.dma_start(Qs[KR:KS, 1 - parity], t["no_shift"][:, 0:4]).then_inc(sem["shift_loaded_0"], 16)
                if fin:
                    store(i - 1)

            step(-1, True, False, False, 1)
            step(0, True, True, False, 0)
            with sp.Fori(0, (B - 2) // 2 - 1) as j:
                step(2 * j + 1, True, True, True, 1)
                step(2 * j + 2, True, True, True, 0)
            step(B - 3, True, True, True, 1)
            step(B - 2, True, True, True, 0, ahead=False)
            step(B - 1, False, True, True, 1)
            step(B, False, False, True, 0)
            sp.wait_ge(sem["out_written"], PER["out_written"] * B)

        @block.tensor
        def _(pe):
            mm = nc.tensor.matmul

            def prepare(a, k, half):
                bank = ps_a
                pe.wait_ge(sem["a_drained"], upto("a_drained", a, k))
                if k < 4:
                    if k == 0:
                        pe.wait_ge(sem["x_loaded"], upto("x_loaded", a, 48))
                    for n, tile in enumerate(pairs[k]):
                        g = 3 if tile == NT - 1 else GR
                        r0 = GR * tile
                        o = bank[0:g * G, n * D:n * D + D]
                        for q, (dr, dc) in enumerate(((0, 0), (0, 1), (1, 0), (1, 1))):
                            last = mm(o, xa[:, dc, G * (r0 + dr):G * (r0 + dr + g)], w_conv[:, q],
                                      start=(q == 0), stop=False, skip_group_check=True)
                        for dr in range(2):
                            last = mm(o, xb[:, G * (r0 + dr):G * (r0 + dr + g)], w_conv[:, 4 + dr],
                                      start=False, stop=(dr == 1), skip_group_check=True)
                    last.then_inc(sem["a_filled"], 1)
                elif k < 8:
                    if k == 4:
                        pe.wait_ge(sem["xn_ready"], upto("xn_ready", a, 1))
                    hf, tiles = quads[k - 4]
                    for n, tile in enumerate(tiles):
                        last = nc.tensor.transpose(bank[0:96, n * TS:n * TS + rows(tile)],
                                                   xn[0:rows(tile), tile, 96 * hf:96 * hf + 96],
                                                   ident[0:rows(tile), 0:rows(tile)])
                    last.then_inc(sem["a_filled"], 1)
                elif k < 16:
                    c, hf = divmod(k - 8, 2)
                    for kk in range(2):
                        last = mm(bank[0:96, 0:HF], w_qk[:, kk, 96 * c:96 * c + 96], xnT[0:96, kk, hf * HF:hf * HF + HF],
                                  start=(kk == 0), stop=(kk == 1))
                    last.then_inc(sem["a_filled"], 1)
                elif k == 17:
                    pe.wait_ge(sem["bound_chain"], upto("bound_chain", a, 3))
                    for c in range(2):
                        last = mm(bank[0:1, 6 * c:6 * c + 6], bound[:, c:c + 1], head_rows[:], start=True, stop=True,
                                  skip_group_check=True)
                    last.then_inc(sem["a_filled"], 1)
                else:
                    for n, tile in enumerate(pairs[v_fill[k]]):
                        for kk in range(2):
                            kp = 96 + kk
                            last = mm(bank[0:TL, n * D:n * D + D], xnT[0:kp, kk, TS * tile:TS * tile + TL],
                                      w_v[0:kp, kk], start=(kk == 0), stop=(kk == 1), skip_group_check=True)
                    last.then_inc(sem["a_filled"], 1)

            def finish(c, k):
                bank = ps_c
                pe.wait_ge(sem["c_drained"], upto("c_drained", c, k))
                if k < 4:
                    if k == 0:
                        pe.wait_ge(sem["o_ready"], upto("o_ready", c, 3))
                    for n, tile in enumerate(pairs[k]):
                        for g in range(NG):
                            last = mm(bank[0:TL, n * D:n * D + D], oT[:, g, TS * tile:TS * tile + TL], w_p[:, g],
                                      start=(g == 0), stop=(g == NG - 1), skip_group_check=True)
                elif k < 8:
                    if k == 4:
                        pe.wait_ge(sem["x2_ready"], upto("x2_ready", c, 1))
                    hf, tiles = quads[k - 4]
                    for n, tile in enumerate(tiles):
                        last = nc.tensor.transpose(bank[0:96, n * TS:n * TS + rows(tile)],
                                                   x2[0:rows(tile), tile, 96 * hf:96 * hf + 96],
                                                   ident[0:rows(tile), 0:rows(tile)])
                elif k < 10:
                    hf = k - 8
                    for kk in range(2):
                        last = mm(bank[0:NS, 0:HF], slots[:, kk], x2T[:, kk, hf * HF:hf * HF + HF],
                                  start=(kk == 0), stop=(kk == 1))
                elif k == 10:
                    for tile in range(NT):
                        for kk in range(2):
                            last = mm(bank[0:TL, tile * NS:tile * NS + NS], x2T[:, kk, TS * tile:TS * tile + TL],
                                      slots[:, kk], start=(kk == 0), stop=(kk == 1), skip_group_check=True)
                elif k == 11:
                    pe.wait_ge(sem["diag_ready"], upto("diag_ready", c, 1))
                    for tile in range(NT):
                        last = mm(bank[0:TL, tile * NS:tile * NS + NS], lT[:, TS * tile:TS * tile + TL], diag[:],
                                  start=True, stop=True, skip_group_check=True)
                elif k < 14:
                    pe.wait_ge(sem["comb_exp"], upto("comb_exp", c, 1))
                    for n, tile in enumerate(quads[k - 12][1]):
                        last = nc.tensor.transpose(bank[0:NS, n * TS:n * TS + rows(tile)], lc[0:rows(tile), tile],
                                                   ident[0:rows(tile), 0:rows(tile)])
                elif k == 14:
                    for hf in range(2):
                        for tile in range(NT):
                            m = rows(tile)
                            last = mm(bank[0:96, hf * NS:hf * NS + NS], x2[0:m, tile, 96 * hf:96 * hf + 96],
                                      disp[0:m, tile], start=(tile == 0), stop=(tile == NT - 1), skip_group_check=True)
                elif k == 15:
                    for m in range(2):
                        for kk in range(2):
                            last = mm(bank[0:96, m * NS:m * NS + NS], w_down[:, kk, 96 * m:96 * m + 96], xt[:, kk],
                                      start=(kk == 0), stop=(kk == 1), skip_group_check=True)
                elif k == 16:
                    pe.wait_ge(sem["hidden_ready"], upto("hidden_ready", c, 1))
                    for m in range(2):
                        last = mm(bank[0:NS, 0:D], hm[:, m], w_up[:, m], start=(m == 0), stop=(m == 1))
                else:
                    for n, tile in enumerate(pairs[k - 17]):
                        last = mm(bank[0:TL, n * D:n * D + D], cT[:, TS * tile:TS * tile + TL], yt[:],
                                  start=True, stop=True, skip_group_check=True)
                last.then_inc(sem["c_filled"], 1)

            def scores(b, unit, heads, half):
                g, tile = divmod(unit, NT)
                for j in heads:
                    n = 4 * unit + j
                    pe.wait_ge(sem["exp_done"], upto("exp_done", b, n - 1))
                    if tile == 0 and j == 0:
                        pe.wait_ge(sem[f"group_loaded_{g}"], upto(f"group_loaded_{g}", b, 192))
                        pe.wait_ge(sem[f"shift_loaded_{g}"], upto(f"shift_loaded_{g}", b, 16))
                    for hf in range(2):
                        last = mm(ps_s[0:rows(tile), n % 2, hf, 0:HF], Ks[:, (half + g) % 2, j, TS * tile:TS * tile + rows(tile)],
                                  Qs[:, (half + g) % 2, j, hf * HF:hf * HF + HF], start=True, stop=True)
                    last.then_inc(sem["s_filled"], 1)

            def weigh(b, unit, half):
                g, tile = divmod(unit, NT)
                m = rows(tile)
                pe.wait_ge(sem["exp_done"], upto("exp_done", b, 4 * unit + 4))
                if unit == 0:
                    pe.wait_ge(sem["a_drained"], upto("a_drained", b, 21))
                if tile == 0:
                    pe.wait_ge(sem["o_ready"], upto("o_ready", b, g))
                for hf in range(2):
                    for j in range(4):
                        last = mm(ps_o[32 * j:32 * j + HD + 1, hf, 0:HF], v[0:m, half, tile, 4 * g + j],
                                  probs[0:m, (half + unit) % 2, j, hf * HF:hf * HF + HF],
                                  start=(tile == 0), stop=(tile == NT - 1), tile_position=(0, 32 * j))
                last.then_inc(sem["pv_done"], 1)

            def maxima(a, half):
                pe.wait_ge(sem["group_loaded_0"], upto("group_loaded_0", a, 192))
                for head in range(NH):
                    g, j = divmod(head, 4)
                    if j == 0 and g:
                        pe.wait_ge(sem["m_loaded"], upto("m_loaded", a, 192 * g))
                    at = half if g == 0 else 1 - half
                    for tile in range(NT):
                        n = head * NT + tile
                        if n >= 2:
                            pe.wait_ge(sem["m_drained"], upto("m_drained", a, n - 1))
                        else:
                            pe.wait_ge(sem["exp_done"], upto("exp_done", a - 1, 84))
                        for hf in range(2):
                            lo = hf * (HF - 1)
                            last = mm(ps_s[0:TL, n % 2, hf, 0:HF], Qs[0:KR, at, j, TS * tile:TS * tile + TL],
                                      Ks[0:KR, at, j, lo:lo + HF], start=True, stop=True)
                        last.then_inc(sem["m_filled"], 1)
                for n, tiles in enumerate(((0, 1, 2, 3), (4, 5, 6))):
                    pe.wait_ge(sem["m_drained"], upto("m_drained", a, 84))
                    for q, tile in enumerate(tiles):
                        last = nc.tensor.transpose(ps_s[0:NH, 0, n, q * TS:q * TS + rows(tile)],
                                                   mx[0:rows(tile), tile], ident[0:rows(tile), 0:rows(tile)])
                    last.then_inc(sem["m_filled"], 1)

            def step(i, prep, att, fin, parity):
                if att:
                    scores(i, 0, range(4), parity)
                for s in range(UNITS):
                    if att and s + 1 < UNITS:
                        scores(i, s + 1, (0, 1), parity)
                    if fin and c_at[s]:
                        finish(i - 1, c_at[s][0])
                    if att and s + 1 < UNITS:
                        scores(i, s + 1, (2, 3), parity)
                    if prep:
                        for k in a_at[s]:
                            prepare(i + 1, k, 1 - parity)
                    if att:
                        weigh(i, s, parity)
                    if fin and len(c_at[s]) > 1:
                        finish(i - 1, c_at[s][1])
                if prep:
                    pe.wait_ge(sem["flag_ready"], upto("flag_ready", i + 1, 1))
                    pe.sem_inc(sem["flag_seen"], 1)
                    with pe.If(pe.value_load(flag[0:1, 1 - parity:2 - parity]) > 0):
                        maxima(i + 1, 1 - parity)
                    with pe.Else():
                        pe.sem_inc(sem["m_filled"], PER["m_filled"])

            pe.wait_ge(setup_done, 1)
            step(-1, True, False, False, 1)
            step(0, True, True, False, 0)
            with pe.Fori(0, (B - 2) // 2) as j:
                step(2 * j + 1, True, True, True, 1)
                step(2 * j + 2, True, True, True, 0)
            step(B - 1, False, True, True, 1)
            step(B, False, False, True, 0)

        @block.scalar
        def _(act):
            def exps(b, unit, half):
                g, tile = divmod(unit, NT)
                m = rows(tile)
                for j in range(4):
                    n = 4 * unit + j
                    act.wait_ge(sem["s_filled"], upto("s_filled", b, n + 1))
                    if j == 0:
                        act.wait_ge(sem["pv_done"], upto("pv_done", b, unit - 1))
                    nc.scalar.activation(probs[0:m, (half + unit) % 2, j].rearrange("p (a n) -> p a n", a=2),
                                         ps_s[0:m, n % 2, :, 0:HF], ACT.Exp).then_inc(sem["exp_done"], 1)

            def guess(b, g):
                act.wait_ge(sem["o_bcast"], upto("o_bcast", b, g + 1))
                nc.scalar.activation(rec[:], den[:], ACT.Ln).then_inc(sem["o_guess"], 1)
                act.wait_ge(sem["o_guess"], upto("o_guess", b, 2 * g + 1))
                nc.scalar.activation(rec[:], rec[:], ACT.Exp, scale=-1.0).then_inc(sem["o_guess"], 1)

            def copy_qk(a, k):
                c, hf = divmod(k - 8, 2)
                act.wait_ge(sem["a_filled"], upto("a_filled", a, k + 1))
                if hf == 0:
                    act.wait_ge(sem["r_ready"], upto("r_ready", a, 2 * (c - 1)))
                nc.scalar.activation(f[:, c % 2, hf * HF:hf * HF + HF], ps_a[0:96, 0:HF], ACT.Identity,
                                     bias=b_qk[:, c:c + 1], scale=HD ** -0.5 if c < 2 else 1.0)\
                    .then_inc(sem["a_drained"], 1)

            def step(i, prep, att, fin, parity):
                if att:
                    exps(i, 0, parity)
                for s in range(UNITS):
                    if att and s + 1 < UNITS:
                        exps(i, s + 1, parity)
                    if prep and 9 <= s < 17:
                        copy_qk(i + 1, a_at[s][0])
                    if fin and s == 10:
                        act.wait_ge(sem["c_chain"], upto("c_chain", i - 1, 3))
                        nc.scalar.activation(lT[:, 0:N], lT[:, 0:N], ACT.Exp, bias=nmax[:], accum_out=dsum[:])\
                            .then_inc(sem["disp_exp"], 1)
                        act.wait_ge(sem["c_drained"], upto("c_drained", i - 1, 11))
                        nc.scalar.activation(lc[:], lc[:], ACT.Exp).then_inc(sem["comb_exp"], 1)
                    if att and s % NT == NT - 1:
                        guess(i, s // NT)

            act.preload_act_table_set("natural_log_exp_and_others")
            act.wait_ge(setup_done, 1)
            step(-1, True, False, False, 1)
            step(0, True, True, False, 0)
            with act.Fori(0, (B - 2) // 2) as j:
                step(2 * j + 1, True, True, True, 1)
                step(2 * j + 2, True, True, True, 0)
            step(B - 1, False, True, True, 1)
            step(B, False, False, True, 0)

        @block.vector
        def _(dve):
            V = nc.vector
            made = [0]

            def link(ins):
                made[0] += 1
                ins.then_inc(setup_dve, 1)
                dve.wait_ge(setup_dve, made[0])

            V.memset(h[:].rearrange("p a t d -> p (a t d)"), 0.0)
            V.memset(xnT[0:96, :, N:NP], 0.0)
            V.memset(xnT[96:97], 1.0)
            V.memset(x2T[:, :, N:NP], 0.0)
            V.memset(Ks[KR:KS].rearrange("p a t d -> p (a t d)"), 1.0)
            V.memset(v[:, :, :, :, HD:HD + 1].rearrange("p a t g d -> p (a t g) d"), 1.0)
            V.memset(ps_o[:], 0.0)
            V.memset(neg[:], 0.0)
            for n, value in enumerate((-0.5, 0.5, -1.0, LN_EPS, L2_EPS, float(D), 0.0)):
                last = V.memset(const[:, n], value)
            link(last)
            dve.wait_ge(params_loaded, 17 * 16)
            V.tensor_tensor(pos[:], pos[:], tokb[:].unsqueeze(1).to_broadcast([TG, NT, D]), ALU.add)
            V.tensor_tensor(cls[:, 0], cls[:, 0], cls[:, 1], ALU.add)
            V.tensor_scalar(b_qk[:, 0:2], b_qk[:, 0:2], HD ** -0.5, None, ALU.mult)
            link(V.tensor_tensor(sq[:], slots[:], slots[:], ALU.mult))
            link(V.tensor_reduce(nrm[:], sq[:].rearrange("p k (e s) -> p k s e", e=NEXP), axis=AX.X, op=ALU.add))
            dve.wait_ge(setup_pool, 1)
            link(V.tensor_scalar(nrm[:], nrm[:], L2_EPS, None, ALU.add))
            link(V.reciprocal(nrm[:], nrm[:]))
            link(V.tensor_scalar(nrm[:], nrm[:], scale_c[:], None, ALU.mult))
            for kk in range(2):
                last = V.tensor_tensor(slots[:, kk].rearrange("p (e s) -> p e s", e=NEXP),
                                       slots[:, kk].rearrange("p (e s) -> p e s", e=NEXP),
                                       nrm[:, kk].unsqueeze(1).to_broadcast([96, NEXP, SLOTS]), ALU.mult)
            last.then_inc(setup_done, 1)
            dve.wait_ge(cls_placed, 32)

            def prepare(a, k, half):
                if not 8 <= k < 16:
                    dve.wait_ge(sem["a_filled"], upto("a_filled", a, k + 1))
                if k < 4:
                    n, t0 = len(pairs[k]), pairs[k][0]
                    m = TG if n == 2 else TGL
                    dve.wait_ge(sem["c_drained"], upto("c_drained", a - 2, k + 1))
                    V.tensor_tensor(h[0:m, half, t0:t0 + n], ps_a[0:m, 0:n * D].rearrange("p (t d) -> p t d", d=D),
                                    pos[0:m, t0:t0 + n], ALU.add).then_inc(sem["a_drained"], 1)
                elif k < 8:
                    hf, tiles = quads[k - 4]
                    c0 = TS * tiles[0]
                    c1 = TS * tiles[-1] + rows(tiles[-1])
                    V.tensor_copy(xnT[0:96, hf, c0:c1], ps_a[0:96, 0:c1 - c0]).then_inc(sem["a_drained"], 1)
                elif k < 16:
                    c, hf = divmod(k - 8, 2)
                    cols = slice(hf * HF, hf * HF + HF)
                    dve.wait_ge(sem["a_drained"], upto("a_drained", a, k + 1))
                    dve.wait_ge(sem[f"parts_written_{c % 2}"], upto(f"parts_written_{c % 2}", a, 16 * (c // 2)))
                    V.tensor_copy(parts[:, c % 2, 0, cols], f[:, c % 2, cols]).then_inc(sem["hi_ready"], 1)
                    V.tensor_reduce(top[:, c, hf:hf + 1], f[:, c % 2, cols], axis=AX.X, op=ALU.max,
                                    apply_absolute_value=True)
                    dve.wait_ge(sem["hi_ready"], upto("hi_ready", a, k - 7))
                    V.tensor_tensor(r[:, c % 2, cols], f[:, c % 2, cols], parts[:, c % 2, 0, cols], ALU.subtract)\
                        .then_inc(sem["r_ready"], 1)
                elif k == 17:
                    V.tensor_reduce(most[:], ps_a[0:1, 0:12], axis=AX.X, op=ALU.max).then_inc(sem["a_drained"], 1)
                    dve.wait_ge(sem["a_drained"], upto("a_drained", a, 18))
                    dve.wait_ge(sem["flag_seen"], upto("flag_seen", a - 1, 0))
                    V.tensor_scalar(flag[0:1, half:half + 1], most[:], LIMIT, None, ALU.is_gt)\
                        .then_inc(sem["flag_ready"], 1)
                else:
                    n, t0 = len(pairs[v_fill[k]]), pairs[v_fill[k]][0]
                    V.tensor_copy(v[:, half, t0:t0 + n, :, 0:HD],
                                  ps_a[0:TL, 0:n * D].rearrange("p (t g d) -> p t g d", g=NH, d=HD))\
                        .then_inc(sem["a_drained"], 1)

            def bounds(a):
                V.memset(held[:, 3:4], 0.0).then_inc(sem["bound_chain"], 1)
                dve.wait_ge(sem["bound_chain"], upto("bound_chain", a, 1))
                V.tensor_tensor(top[:, :, 0], top[:, :, 0], top[:, :, 1], ALU.max).then_inc(sem["bound_chain"], 1)
                dve.wait_ge(sem["bound_chain"], upto("bound_chain", a, 2))
                V.tensor_tensor(bound[:], top[:, 0:2, 0], top[:, 2:4, 0], ALU.mult).then_inc(sem["bound_chain"], 1)

            def carry(n):
                V.memset(held[:, n:n + 1], 0.0)

            def stats(src, into, agg, chain, image):
                for tile in range(NT):
                    last = V.bn_stats(into[:, tile], src[:, tile])
                last.then_inc(sem[chain], 1)
                dve.wait_ge(sem[chain], upto(chain, image, 1))
                carry(0)
                for tile in range(NT):
                    last = V.bn_aggr(agg[:, tile], into[:, tile])
                last.then_inc(sem[chain], 1)

            def normalise(dst, src, agg, factor, ready):
                for tile in range(NT):
                    last = V.tensor_scalar(dst[:, tile], src[:, tile], agg[:, tile, 0:1], factor[:, tile:tile + 1],
                                           ALU.subtract, ALU.mult)
                last.then_inc(sem[ready], 1)

            def maxima(a):
                for n in range(TILES):
                    head, tile = divmod(n, NT)
                    dve.wait_ge(sem["m_filled"], upto("m_filled", a, n + 1))
                    V.tensor_reduce(mx[:, tile, head:head + 1], ps_s[0:TL, n % 2, :, 0:HF], axis=AX.XY, op=ALU.max)\
                        .then_inc(sem["m_drained"], 1)
                dve.wait_ge(sem["shift_written"], upto("shift_written", a, 0))
                dve.wait_ge(sem["m_filled"], upto("m_filled", a, 86))
                V.tensor_scalar(neg[:, 0:4 * TS], ps_s[0:NH, 0, 0, 0:4 * TS], -1.0, None, ALU.mult)
                V.tensor_scalar(neg[:, 4 * TS:N], ps_s[0:NH, 0, 1, 0:N - 4 * TS], -1.0, None, ALU.mult)\
                    .then_inc(sem["m_chain"], 1)
                dve.wait_ge(sem["m_chain"], upto("m_chain", a, 1))
                V.tensor_copy(shift[:, 0], neg[:]).then_inc(sem["m_chain"], 1)
                dve.wait_ge(sem["m_chain"], upto("m_chain", a, 2))
                V.tensor_tensor(shift[:, 1], neg[:], shift[:, 0], ALU.subtract).then_inc(sem["shift_ready"], 1)

            def divide(b, g):
                dve.wait_ge(sem["pv_done"], upto("pv_done", b, NT * (g + 1)))
                dve.wait_ge(sem["c_filled"], upto("c_filled", b - 1, 4))
                dve.wait_ge(sem["o_ready"], upto("o_ready", b, g))
                carry(2)
                V.stream_shuffle(den[:].rearrange("p (a n) -> p a n", a=2), ps_o[:, :, 0:HF], [HD] * 32)\
                    .then_inc(sem["o_bcast"], 1)
                dve.wait_ge(sem["o_guess"], upto("o_guess", b, 2 * g + 2))
                V.tensor_tensor(den[:], den[:], rec[:], ALU.mult).then_inc(sem["o_chain"], 1)
                dve.wait_ge(sem["o_chain"], upto("o_chain", b, 2 * g + 1))
                V.scalar_tensor_tensor(den[:], den[:], 2.0, rec[:], ALU.subtract, ALU.mult)\
                    .then_inc(sem["o_chain"], 1)
                dve.wait_ge(sem["o_chain"], upto("o_chain", b, 2 * g + 2))
                V.scalar_tensor_tensor(oT[:, g].rearrange("p (a n) -> p a n", a=2), ps_o[:, :, 0:HF], -1.0,
                                       den[:].rearrange("p (a n) -> p a n", a=2), ALU.mult, ALU.mult)\
                    .then_inc(sem["o_ready"], 1)

            step_count = [0]

            def chain(ins, c):
                step_count[0] += 1
                ins.then_inc(sem["c_chain"], 1)
                dve.wait_ge(sem["c_chain"], upto("c_chain", c, step_count[0]))

            def finish(c, k, half):
                dve.wait_ge(sem["c_filled"], upto("c_filled", c, k + 1))
                drained = lambda ins: ins.then_inc(sem["c_drained"], 1)
                if k < 4:
                    n, t0 = len(pairs[k]), pairs[k][0]
                    drained(V.tensor_tensor(h2[:, t0:t0 + n], ps_c[0:TL, 0:n * D].rearrange("p (t d) -> p t d", d=D),
                                            h[:, half, t0:t0 + n], ALU.add))
                elif k < 8:
                    hf, tiles = quads[k - 4]
                    c0 = TS * tiles[0]
                    c1 = TS * tiles[-1] + rows(tiles[-1])
                    drained(V.tensor_copy(x2T[:, hf, c0:c1], ps_c[0:96, 0:c1 - c0]))
                elif k < 10:
                    c0, c1 = (0, HF) if k == 8 else (HF, N)
                    drained(V.tensor_copy(lT[:, c0:c1], ps_c[0:NS, 0:c1 - c0]))
                    if k == 9:
                        dve.wait_ge(sem["c_drained"], upto("c_drained", c, 10))
                        chain(V.tensor_reduce(nmax[:], lT[:, 0:N], axis=AX.X, op=ALU.max, negate=True), c)
                elif k == 10:
                    logits = ps_c[0:TL, 0:NT * NS].rearrange("p (t s) -> p t s", s=NS)
                    chain(V.tensor_reduce(cmax[:], logits, axis=AX.X, op=ALU.max), c)
                    drained(V.tensor_tensor(lc[:], logits, cmax[:].unsqueeze(2).to_broadcast([TL, NT, NS]),
                                            ALU.subtract))
                elif k == 11:
                    drained(V.tensor_copy(disp[:].rearrange("p t s -> p (t s)"), ps_c[0:TL, 0:NT * NS]))
                elif k < 14:
                    tiles = quads[k - 12][1]
                    c0 = TS * tiles[0]
                    c1 = TS * tiles[-1] + rows(tiles[-1])
                    drained(V.tensor_copy(cT[:, c0:c1], ps_c[0:NS, 0:c1 - c0]))
                elif k == 14:
                    drained(V.tensor_copy(xt[:].rearrange("p a s -> p (a s)"), ps_c[0:96, 0:2 * NS]))
                elif k == 15:
                    drained(V.tensor_tensor(u[:], ps_c[0:96, 0:2 * NS].rearrange("p (a s) -> p a s", s=NS),
                                            b_down[:].unsqueeze(2).to_broadcast([96, 2, NS]), ALU.add))
                    dve.wait_ge(sem["c_drained"], upto("c_drained", c, 16))
                    gelu(c)
                elif k == 16:
                    drained(V.tensor_tensor(yt[:], ps_c[0:NS, 0:D], b_up[:], ALU.add))
                else:
                    if k == 17:
                        dve.wait_ge(sem["out_written"], upto("out_written", c, 0))
                    for n, tile in enumerate(pairs[k - 17]):
                        last = V.scalar_tensor_tensor(y[:, tile], ps_c[0:TL, n * D:n * D + D], crec[:, tile:tile + 1],
                                                      h2[:, tile], ALU.mult, ALU.add)
                    drained(last)

            def weights(c):
                dve.wait_ge(sem["disp_exp"], upto("disp_exp", c, 1))
                chain(V.reciprocal(drec[:], dsum[:]), c)
                V.tensor_scalar(diag[:], ident[0:NS, 0:NS], drec[:], None, ALU.mult).then_inc(sem["diag_ready"], 1)
                dve.wait_ge(sem["comb_exp"], upto("comb_exp", c, 1))
                chain(V.tensor_reduce(csum[:], lc[:], axis=AX.X, op=ALU.add), c)
                chain(V.reciprocal(crec[:], csum[:]), c)

            def gelu(c):
                chain(V.tensor_scalar(uc[:], u[:], 0.5 ** 0.5, ERF_MAX, ALU.mult, ALU.min), c)
                chain(V.tensor_scalar(uc[:], uc[:], -ERF_MAX, None, ALU.max), c)
                chain(V.tensor_tensor(u2[:], uc[:], uc[:], ALU.mult), c)
                chain(V.tensor_scalar(pn[:], u2[:], ERF_NUM[0], None, ALU.mult), c)
                for coef in ERF_NUM[1:-1]:
                    chain(V.scalar_tensor_tensor(pn[:], pn[:], coef, u2[:], ALU.add, ALU.mult), c)
                chain(V.scalar_tensor_tensor(pn[:], pn[:], ERF_NUM[-1], uc[:], ALU.add, ALU.mult), c)
                chain(V.tensor_scalar(pd[:], u2[:], ERF_DEN[0], None, ALU.mult), c)
                for coef in ERF_DEN[1:-1]:
                    chain(V.scalar_tensor_tensor(pd[:], pd[:], coef, u2[:], ALU.add, ALU.mult), c)
                chain(V.tensor_scalar(pd[:], pd[:], ERF_DEN[-1], None, ALU.add), c)
                chain(V.reciprocal(pd[:], pd[:]), c)
                chain(V.tensor_tensor(pn[:], pn[:], pd[:], ALU.mult), c)
                chain(V.scalar_tensor_tensor(pn[:], pn[:], 1.0, u[:], ALU.add, ALU.mult), c)
                V.scalar_tensor_tensor(hm[:], pn[:], 0.5, mask[:], ALU.mult, ALU.mult).then_inc(sem["hidden_ready"], 1)

            def step(i, prep, att, fin, parity):
                step_count[0] = 0
                for s in range(UNITS):
                    if fin:
                        if s == 4:
                            dve.wait_ge(sem["ln2_pool"], upto("ln2_pool", i - 1, 8))
                            normalise(x2, h2, mv2, sc2, "x2_ready")
                        if s == 11:
                            weights(i - 1)
                        for k in c_at[s][:1]:
                            finish(i - 1, k, 1 - parity)
                        if s == 3:
                            dve.wait_ge(sem["c_drained"], upto("c_drained", i - 1, 4))
                            for tile in range(NT):
                                last = V.bn_stats(st2[:, tile], h2[:, tile])
                            chain(last, i - 1)
                            carry(1)
                            for tile in range(NT):
                                last = V.bn_aggr(mv2[:, tile], st2[:, tile])
                            chain(last, i - 1)
                    if prep:
                        if s == 4:
                            dve.wait_ge(sem["ln1_pool"], upto("ln1_pool", i + 1, 2))
                            normalise(xn, h[:, 1 - parity], mv, rstd, "xn_ready")
                        for k in a_at[s]:
                            prepare(i + 1, k, 1 - parity)
                        if s == 16:
                            bounds(i + 1)
                        if s == 3:
                            dve.wait_ge(sem["a_drained"], upto("a_drained", i + 1, 4))
                            dve.wait_ge(sem["txt_loaded"], upto("txt_loaded", i + 1, 32))
                            stats(h[:, 1 - parity], st, mv, "a_chain", i + 1)
                    if att and s % NT == NT - 1:
                        divide(i, s // NT)
                    if fin:
                        for k in c_at[s][1:]:
                            finish(i - 1, k, 1 - parity)
                if fin:
                    assert step_count[0] == PER["c_chain"], step_count
                if prep:
                    dve.wait_ge(sem["flag_ready"], upto("flag_ready", i + 1, 1))
                    dve.sem_inc(sem["flag_seen"], 1)
                    with dve.If(dve.value_load(flag[0:1, 1 - parity:2 - parity]) > 0):
                        maxima(i + 1)
                    with dve.Else():
                        dve.sem_inc(sem["m_drained"], PER["m_drained"])
                        dve.sem_inc(sem["m_chain"], PER["m_chain"])
                        dve.sem_inc(sem["shift_ready"], PER["shift_ready"])

            step(-1, True, False, False, 1)
            step(0, True, True, False, 0)
            with dve.Fori(0, (B - 2) // 2) as j:
                step(2 * j + 1, True, True, True, 1)
                step(2 * j + 2, True, True, True, 0)
            step(B - 1, False, True, True, 1)
            step(B, False, False, True, 0)

        @block.gpsimd
        def _(pool):
            G_ = nc.gpsimd
            pool.wait_ge(setup_dve, 3)
            G_.tensor_tensor(nrm[:].rearrange("p a s -> p (a s)"), nrm[:].rearrange("p a s -> p (a s)"),
                             const[0:96, 1, 0:2 * SLOTS], ALU.pow).then_inc(setup_pool, 1)

            def layernorm1(a):
                pool.wait_ge(sem["a_chain"], upto("a_chain", a, 2))
                G_.tensor_tensor(ve[:, 0:NT], mv[:, :, 1], const[0:TL, 3, 0:NT], ALU.add).then_inc(sem["ln1_pool"], 1)
                pool.wait_ge(sem["ln1_pool"], upto("ln1_pool", a, 1))
                G_.tensor_tensor(rstd[:, 0:NT], ve[:, 0:NT], const[0:TL, 0, 0:NT], ALU.pow).then_inc(sem["ln1_pool"], 1)

            def layernorm2(c):
                ops = [
                    lambda: G_.tensor_tensor(ve2[:, 0:NT], mv2[:, :, 1], const[0:TL, 3, 0:NT], ALU.add),
                    lambda: G_.tensor_tensor(rstd2[:, 0:NT], ve2[:, 0:NT], const[0:TL, 0, 0:NT], ALU.pow),
                    lambda: G_.tensor_tensor(nr2[:, 0:NT], mv2[:, :, 1], const[0:TL, 5, 0:NT], ALU.mult),
                    lambda: G_.tensor_tensor(nr2[:, 0:NT], nr2[:, 0:NT], const[0:TL, 1, 0:NT], ALU.pow),
                    lambda: G_.tensor_tensor(nr2[:, 0:NT], nr2[:, 0:NT], rstd2[:, 0:NT], ALU.mult),
                    lambda: G_.tensor_tensor(nr2[:, 0:NT], nr2[:, 0:NT], const[0:TL, 4, 0:NT], ALU.add),
                    lambda: G_.tensor_tensor(nr2[:, 0:NT], nr2[:, 0:NT], const[0:TL, 2, 0:NT], ALU.pow),
                    lambda: G_.tensor_tensor(sc2[:, 0:NT], rstd2[:, 0:NT], nr2[:, 0:NT], ALU.mult),
                ]
                pool.wait_ge(sem["c_chain"], upto("c_chain", c, 2))
                for n, op in enumerate(ops):
                    pool.wait_ge(sem["ln2_pool"], upto("ln2_pool", c, n))
                    op().then_inc(sem["ln2_pool"], 1)

            def split(a, c):
                pool.wait_ge(sem["r_ready"], upto("r_ready", a, 2 * c + 2))
                G_.tensor_tensor(parts[:, c % 2, 1], r[:, c % 2], const[0:96, 6, 0:1].to_broadcast([96, NP]), ALU.add).then_inc(sem["mid_ready"], 1)
                pool.wait_ge(sem["mid_ready"], upto("mid_ready", a, c + 1))
                G_.tensor_tensor(parts[:, c % 2, 2], r[:, c % 2], parts[:, c % 2, 1], ALU.subtract)\
                    .then_inc(sem["parts_ready"], 1)

            def step(i, prep, att, fin, parity):
                if fin:
                    layernorm2(i - 1)
                if prep:
                    layernorm1(i + 1)
                    for c in range(4):
                        split(i + 1, c)

            step(-1, True, False, False, 1)
            step(0, True, True, False, 0)
            with pool.Fori(0, (B - 2) // 2) as j:
                step(2 * j + 1, True, True, True, 1)
                step(2 * j + 2, True, True, True, 0)
            step(B - 1, False, True, True, 1)
            step(B, False, False, True, 0)


def kernel(**inputs):
    import numpy as np
    import concourse.bacc as bacc
    from concourse.bass_utils import run_bass_kernel_spmd

    inp = {k: np.asarray(v) for k, v in inputs.items()}
    f32, bf16 = np.float32, mybir.dt.np(BF16)
    B = inp["x"].shape[0]
    blocks = inp["x"].reshape(B, C, BG, S, BG, S).transpose(0, 1, 3, 5, 2, 4).reshape(B, C * S * S, BG, BG)
    x = np.stack([blocks[..., :G], blocks[..., 1:]], axis=1).reshape(B, 2, C * S * S, BG * G)
    w = inp["L0_tok_w"].reshape(D, C, 2, S, 2, S).transpose(2, 4, 1, 3, 5, 0).reshape(2, 2, C * S * S, D)
    w_conv = np.stack([w[0, 0, :128], w[0, 1, :128], w[1, 0, :128], w[1, 1, :128],
                       np.concatenate([w[0, 0, 128:], w[0, 1, 128:]]),
                       np.concatenate([w[1, 0, 128:], w[1, 1, 128:]])], axis=1)
    qkv = inp["L0_attn_qkv_w"].T.reshape(2, 96, 3 * D).transpose(1, 0, 2)
    qkv_b = inp["L0_attn_qkv_b"]
    w_v = np.zeros((97, 2, D), f32)
    w_v[:96] = qkv[:, :, 2 * D:]
    w_v[96, 1] = qkv_b[2 * D:]
    w_p = np.zeros((NG, 4, 32, D), f32)
    w_p[:, :, :HD] = inp["L0_attn_proj_w"].T.reshape(NG, 4, HD, D)
    w_p[0, 0, HD] = inp["L0_attn_proj_b"]
    position = inp["L0_tok_pos_embedding"][0]
    pos = np.zeros((TG, NT, D), f32)
    pos[:, :NT - 1] = position[1:1 + TG * (NT - 1)].reshape(NT - 1, TG, D).transpose(1, 0, 2)
    pos[:TGL, NT - 1] = position[1 + TG * (NT - 1):]
    halves = lambda a: a.reshape(2, 96, -1).transpose(1, 0, 2)
    expert = np.arange(NEXP * HID) // HID
    arrays = {
        "x": x, "txt": inp["txt"], "w_conv": w_conv,
        "w_qk": qkv[:, :, :2 * D], "b_qk": qkv_b[:2 * D].reshape(4, 96).T, "w_v": w_v,
        "w_p": w_p.reshape(NG, 128, D).transpose(1, 0, 2), "pos": pos, "tok_b": inp["L0_tok_b"],
        "cls": np.concatenate([inp["L0_tok_cls_token"].reshape(1, 1, D), position[:1][None]], axis=1),
        "slots": halves(inp["L0_ffn_slot_params"].reshape(D, NS)),
        "slot_scale": inp["L0_ffn_scale"].reshape(1),
        "w_down": halves(inp["L0_ffn_W_down"].transpose(1, 0, 2).reshape(D, D)),
        "b_down": inp["L0_ffn_b_down"].reshape(2, 96).T,
        "w_up": halves(inp["L0_ffn_W_up"].reshape(D, D)),
        "b_up": np.repeat(inp["L0_ffn_b_up"], SLOTS, axis=0),
        "head_rows": np.repeat(np.eye(6, dtype=f32), HD, axis=0), "no_shift": np.zeros((2, NH, NP), bf16),
        "ident": np.eye(128, dtype=f32),
        "expert_mask": halves((expert[:, None] == np.arange(NS)[None] // SLOTS).astype(f32)),
    }
    arrays = {f"in_{k}": np.ascontiguousarray(v) for k, v in arrays.items()}
    nc = bacc.Bacc("TRN2", target_bir_lowering=False, num_devices=1)
    nc.disable_value_cache = True
    t = {k[3:]: nc.dram_tensor(k, v.shape, mybir.dt.from_np(v.dtype), kind="ExternalInput").ap()
         for k, v in arrays.items()}
    scr_parts = nc.dram_tensor("scr_parts", [4, 96, 3, NP], BF16, kind="Internal").ap()
    scr_shift = nc.dram_tensor("scr_shift", [2, NH, NP], BF16, kind="Internal").ap()
    out = nc.dram_tensor("out", [B, N, D], F32, kind="ExternalOutput").ap()
    early_fusion(nc, B, t, scr_parts, scr_shift, out)
    got = run_bass_kernel_spmd(nc, [arrays], core_ids=[0])
    return got.results[0]["out"]
```

```python
from contextlib import ExitStack

import concourse.bass as bass
from concourse import mybir

ALU = mybir.AluOpType
ACT = mybir.ActivationFunctionType
AX = mybir.AxisListType
F32 = mybir.dt.float32
BF16 = mybir.dt.bfloat16

C, IMG, P, S, D = 3, 224, 16, 8, 192
G = (IMG - P) // S + 1
BG = IMG // S
TXT = 77
NH, HD = 12, 16
NEXP, SLOTS, HID = 8, 4, 24
NS = NEXP * SLOTS
N = G * G + 1 + TXT
NT = 7
GR = 4
TG = GR * G
TGL = G * G - (NT - 1) * TG
TX = 7
TS = TG + TX
TL = N - (NT - 1) * TS
NP = N + 1
HF = NP // 2
KB = 6
KR = KB * HD
KS = KR + 2
NG = NH // 4
UNITS = NG * NT
TILES = UNITS * 4
Q_PARTS = (0, 0, 1, 1, 0, 2)
K_PARTS = (0, 1, 0, 1, 2, 0)
LN_EPS, L2_EPS = 1e-5, 1e-6
LIMIT = 36.0
ERF_NUM = (0.00022905065861350646, 0.0034082910107109506, 0.050955695062380861, 0.18520832239976145,
           1.128379143519084)
ERF_DEN = (-1.1791602954361697e-7, 0.000023547966471313185, 0.0010179625278914885, 0.014070470171167667,
           0.11098505178285362, 0.49746925110067538, 1.0)
ERF_MAX = 3.7439211627767994

PER = dict(
    x_loaded=48, txt_loaded=32, a_filled=24, a_drained=24, stats_done=7, a_chain=1, bound_chain=2, flag_ready=1, flag_seen=3, ln1_pool=2, xn_ready=1,
    hi_ready=8, r_ready=8, mid_ready=4, parts_ready=4, parts_written_0=32, parts_written_1=32,
    group_loaded_0=192, group_loaded_1=192, group_loaded_2=192, m_loaded=384, shift_written=16,
    shift_loaded_0=16, shift_loaded_1=16, shift_loaded_2=16, s_filled=84, exp_done=84, pv_done=42, o_copied=6, o_bcast=6, o_guess=6, o_chain=6, o_ready=3,
    m_filled=86, m_drained=84, m_chain=2, shift_ready=1,
    c_filled=21, c_drained=21, c_chain=23, stats2_done=4, ln2_chain=5, ln2_pool=3, x2_ready=1, disp_exp=1, comb_exp=1, diag_ready=1,
    hidden_ready=1, out_written=80,
)


def early_fusion(nc, B, t, scr_parts, scr_shift, out):
    with ExitStack() as ctx:
        def sb(name, shape, dt=F32):
            return ctx.enter_context(nc.sbuf_tensor(name, shape, dt))

        sem = {name: ctx.enter_context(nc.semaphore(name)) for name in PER}
        params_loaded = ctx.enter_context(nc.semaphore("params_loaded"))
        cls_placed = ctx.enter_context(nc.semaphore("cls_placed"))
        setup_dve = ctx.enter_context(nc.semaphore("setup_dve"))
        setup_pool = ctx.enter_context(nc.semaphore("setup_pool"))
        setup_done = ctx.enter_context(nc.semaphore("setup_done"))

        w_conv = sb("w_conv_sb", [128, 6, D])
        w_qk = sb("w_qk_sb", [96, 2, 4 * 96])
        b_qk = sb("b_qk_sb", [96, 4])
        w_v = sb("w_v_sb", [97, 2, D])
        w_p = sb("w_p_sb", [128, NG, D])
        pos = sb("pos_sb", [TG, NT, D])
        slots = sb("slots_sb", [96, 2, NS])
        w_down = sb("w_down_sb", [96, 2, D])
        b_down = sb("b_down_sb", [96, 2])
        w_up = sb("w_up_sb", [96, 2, D])
        b_up = sb("b_up_sb", [NS, D])
        ident = sb("ident_sb", [128, 128])
        mask = sb("mask_sb", [96, 2, NS])
        cls = sb("cls_sb", [1, 2, D])
        tokb = sb("tokb_sb", [TG, D])
        scale_c = sb("scale_c", [96, 1])
        sq = sb("sq", [96, 2, NS])
        nrm = sb("nrm", [96, 2, SLOTS])
        const = sb("const", [128, 7, 8])
        held = sb("held", [1, 8])

        xa = sb("xa_sb", [128, 2, BG * G])
        xb = sb("xb_sb", [128, BG * G])
        h = sb("h", [TL, 2, NT, D])
        xn = sb("xn", [TL, NT, D])
        xnT = sb("xnT", [97, 2, NP])
        st = sb("st", [TL, NT, 6])
        mv = sb("mv", [TL, NT, 2])
        ve = sb("ve", [TL, 8])
        rstd = sb("rstd", [TL, 8])
        f = sb("f", [96, 2, NP])
        r = sb("r", [96, 2, NP])
        parts = sb("parts", [96, 2, 3, NP], BF16)
        Qs = sb("Qs", [KS, 2, 4, NP], BF16)
        Ks = sb("Ks", [KS, 2, 4, NP], BF16)
        v = sb("v", [TL, 2, NT, NH, HD + 1])
        top = sb("top", [96, 4, 2])
        bound = sb("bound", [96, 2])
        most = sb("most", [1, 1])
        flag = sb("flag", [1, 2], mybir.dt.int32)
        head_rows = sb("head_rows_sb", [96, 6])
        mx = sb("mx", [TL, NT, NH])
        neg = sb("neg", [NH, NP])
        shift = sb("shift", [NH, 2, NP], BF16)
        probs = sb("probs", [TL, 2, 4, NP])
        den = sb("den", [128, NP])
        rec = sb("rec", [128, NP])
        oT = sb("oT", [128, NG, NP])
        h2 = sb("h2", [TL, NT, D])
        x2 = sb("x2", [TL, NT, D])
        x2T = sb("x2T", [96, 2, NP])
        st2 = sb("st2", [TL, NT, 6])
        mv2 = sb("mv2", [TL, NT, 2])
        ve2 = sb("ve2", [TL, 2, 8])
        pow2 = sb("pow2", [TL, 2, 8])
        sc2 = sb("sc2", [TL, 2, 8])
        lT = sb("lT", [NS, NP])
        nmax = sb("nmax", [NS, 1])
        dsum = sb("dsum", [NS, 1])
        drec = sb("drec", [NS, 1])
        diag = sb("diag", [NS, NS])
        lc = sb("lc", [TL, NT, NS])
        cmax = sb("cmax", [TL, NT])
        csum = sb("csum", [TL, NT])
        crec = sb("crec", [TL, NT])
        disp = sb("disp", [TL, NT, NS])
        cT = sb("cT", [NS, NP])
        xt = sb("xt", [96, 2, NS])
        u = sb("u", [96, 2, NS])
        uc = sb("uc", [96, 2, NS])
        u2 = sb("u2", [96, 2, NS])
        pn = sb("pn", [96, 2, NS])
        pd = sb("pd", [96, 2, NS])
        hm = sb("hm", [96, 2, NS])
        yt = sb("yt", [NS, D])
        y = sb("y", [TL, NT, D])

        ps_s = ctx.enter_context(nc.psum_tensor("ps_s", [128, 2, 2, 512], F32))
        ps_o = ctx.enter_context(nc.psum_tensor("ps_o", [128, 2, 512], F32))
        ps_a = ctx.enter_context(nc.psum_tensor("ps_a", [128, 512], F32))
        ps_c = ctx.enter_context(nc.psum_tensor("ps_c", [128, 512], F32))

        def upto(name, image, count):
            value = image * PER[name] + count
            return max(value, 0) if isinstance(value, int) else value

        def rows(tile):
            return TL if tile == NT - 1 else TS

        FILLS = {2: ("proj", 0), 3: ("conv", 0), 4: ("conv", 1), 5: ("proj", 1), 6: ("conv", 2), 8: ("proj", 2),
                 9: ("conv", 3), 11: ("proj", 3), 12: ("conv", 4), 14: ("conv", 5), 16: ("conv", 6),
                 17: ("x2T", 0), 18: ("x2T", 1), 19: ("x2T", 2), 20: ("x2T", 3), 21: ("lT", 0), 22: ("lT", 1),
                 23: ("logits", 0), 24: ("xnT", 0), 25: ("xnT", 1), 26: ("xnT", 2), 27: ("xnT", 3),
                 **{29 + 4 * n: ("qk", n) for n in range(8)},
                 31: ("disp", 0), 34: ("cT", 0), 35: ("xt", 0), 38: ("cT", 1), 39: ("hidden", 0), 48: ("yt", 0),
                 52: ("y", 0), 58: ("y", 1), 64: ("y", 2), 70: ("y", 3),
                 61: ("v", 0), 66: ("v", 1), 68: ("bound", 0), 72: ("v", 2), 78: ("v", 3)}
        PREPARES = ("conv", "xnT", "qk", "v", "bound")
        AT = {fill: quarter for quarter, fill in FILLS.items()}
        a_order = [FILLS[q] for q in sorted(FILLS) if FILLS[q][0] in PREPARES]
        c_order = [FILLS[q] for q in sorted(FILLS) if FILLS[q][0] not in PREPARES]
        a_nth = {fill: n + 1 for n, fill in enumerate(a_order)}
        c_nth = {fill: n + 1 for n, fill in enumerate(c_order)}
        assert len(a_order) == PER["a_filled"] and len(c_order) == PER["c_filled"]
        pairs = [(0, 1), (2, 3), (4, 5), (6,)]
        quads = [(half, ts) for half in range(2) for ts in ((0, 1, 2, 3), (4, 5, 6))]

        block = ctx.enter_context(nc.Block())

        @block.sync
        def _(sp):
            load = lambda dst, src: sp.dma_start(dst, src).then_inc(params_loaded, 16)
            load(w_conv[:], t["w_conv"])
            load(w_qk[:], t["w_qk"])
            load(b_qk[:], t["b_qk"])
            load(w_v[:], t["w_v"])
            load(pos[:], t["pos"])
            load(tokb[:], t["tok_b"].partition_broadcast(TG))
            load(cls[:, :, :], t["cls"])
            load(ident[:], t["ident"])
            load(w_p[:], t["w_p"])
            load(slots[:], t["slots"])
            load(scale_c[:], t["slot_scale"].partition_broadcast(96))
            load(w_down[:], t["w_down"])
            load(b_down[:], t["b_down"])
            load(w_up[:], t["w_up"])
            load(b_up[:], t["b_up"])
            load(mask[:], t["expert_mask"])
            load(head_rows[:], t["head_rows"])

            def load_x(a):
                sp.wait_ge(sem["a_filled"], upto("a_filled", a - 1, a_nth["conv", NT - 1]))
                src = t["x"][bass.ds(a, 1)].rearrange("a s p n -> p (a s) n")
                sp.dma_start(xa[:], src[0:128]).then_inc(sem["x_loaded"], 16)
                sp.dma_start(xb[0:64], src[128:192, 0]).then_inc(sem["x_loaded"], 16)
                sp.dma_start(xb[64:128], src[128:192, 1]).then_inc(sem["x_loaded"], 16)

            def load_txt(a, half):
                if not isinstance(a, int) or a >= 2:
                    sp.wait_ge(sem["c_drained"], upto("c_drained", a - 2, c_nth["proj", 3]))
                src = t["txt"][bass.ds(a, 1)].rearrange("a n d -> (a n) d")
                sp.dma_start(h[TG:TS, half, 0:NT - 1, :],
                             src[0:TX * (NT - 1)].rearrange("(t r) d -> r t d", r=TX)).then_inc(sem["txt_loaded"], 16)
                sp.dma_start(h[TGL + 1:TL, half, NT - 1, :], src[TX * (NT - 1):]).then_inc(sem["txt_loaded"], 16)

            def write_parts(a):
                for c in range(4):
                    if c == 0:
                        sp.wait_ge(sem["group_loaded_2"], upto("group_loaded_2", a, 0))
                    sp.wait_ge(sem["parts_ready"], upto("parts_ready", a, c + 1))
                    sp.dma_start(scr_parts[c], parts[:, c % 2])\
                        .then_inc(sem[f"parts_written_{c % 2}"], 16)

            def load_group(g, half, signal):
                for first, dst, which in ((0, Qs, Q_PARTS), (2, Ks, K_PARTS)):
                    src = scr_parts[first:first + 2].rearrange("c (h d) s n -> d (c h) s n", d=HD)
                    for b, part in enumerate(which):
                        sp.dma_start(dst[HD * b:HD * b + HD, half], src[:, 4 * g:4 * g + 4, part])\
                            .then_inc(sem[signal], 16)

            def load_shift(g, half):
                sp.dma_start(Qs[KR:KS, half], scr_shift[:, 4 * g:4 * g + 4])\
                    .then_inc(sem[f"shift_loaded_{g}"], 16)

            def load_for_maxima(a, half):
                for g in (1, 2):
                    if g == 1:
                        sp.wait_ge(sem["s_filled"], upto("s_filled", a, 0))
                    else:
                        sp.wait_ge(sem["m_filled"], upto("m_filled", a, 56))
                    load_group(g, half, "m_loaded")

            def send_shift(a, half):
                sp.wait_ge(sem["shift_ready"], upto("shift_ready", a, 1))
                sp.dma_start(scr_shift.rearrange("s h n -> h s n"), shift[:]).then_inc(sem["shift_written"], 16)
                sp.wait_ge(sem["shift_written"], upto("shift_written", a, 16))
                load_shift(0, half)

            def store(c):
                dst = out[bass.ds(c, 1)].rearrange("a n d -> (a n) d")
                sp.wait_ge(sem["c_drained"], upto("c_drained", c, c_nth["y", 3]))
                put = lambda d, s: sp.dma_start(d, s).then_inc(sem["out_written"], 16)
                put(dst[1:1 + TG * (NT - 1)].rearrange("(t p) d -> p t d", p=TG), y[0:TG, 0:NT - 1])
                put(dst[1 + TG * (NT - 1):1 + G * G], y[0:TGL, NT - 1])
                put(dst[0:1], y[TGL:TGL + 1, NT - 1])
                put(dst[1 + G * G:1 + G * G + TX * (NT - 1)].rearrange("(t r) d -> r t d", r=TX), y[TG:TS, 0:NT - 1])
                put(dst[1 + G * G + TX * (NT - 1):N], y[TGL + 1:TL, NT - 1])

            load_x(0)
            sp.wait_ge(setup_done, 1)
            for half in range(2):
                sp.dma_start(h[TGL:TGL + 1, half, NT - 1, :], cls[0:1, 0, :]).then_inc(cls_placed, 16)

            def step(i, prep, att, fin, parity, ahead=True):
                if att:
                    sp.wait_ge(sem["s_filled"], upto("s_filled", i, 0))
                    sp.wait_ge(sem["m_filled"], upto("m_filled", i, 84))
                    sp.wait_ge(sem["shift_written"], upto("shift_written", i, 16))
                    load_group(1, 1 - parity, "group_loaded_1")
                    load_shift(1, 1 - parity)
                if prep:
                    load_txt(i + 1, 1 - parity)
                    if ahead:
                        load_x(i + 2)
                if att:
                    sp.wait_ge(sem["s_filled"], upto("s_filled", i, 28))
                    load_group(2, parity, "group_loaded_2")
                    load_shift(2, parity)
                if prep:
                    write_parts(i + 1)
                    sp.wait_ge(sem["s_filled"], upto("s_filled", i, 56))
                    for c in range(2):
                        sp.wait_ge(sem[f"parts_written_{c}"], upto(f"parts_written_{c}", i + 1, 32))
                    load_group(0, 1 - parity, "group_loaded_0")
                if prep:
                    sp.wait_ge(sem["flag_ready"], upto("flag_ready", i + 1, 1))
                    sp.sem_inc(sem["flag_seen"], 1)
                    with sp.If(sp.value_load(flag[0:1, 1 - parity:2 - parity]) > 0):
                        load_for_maxima(i + 1, parity)
                        send_shift(i + 1, 1 - parity)
                    with sp.Else():
                        sp.sem_inc(sem["m_loaded"], PER["m_loaded"])
                        sp.dma_start(scr_shift, t["no_shift"]).then_inc(sem["shift_written"], 16)
                        sp.dma_start(Qs[KR:KS, 1 - parity], t["no_shift"][:, 0:4]).then_inc(sem["shift_loaded_0"], 16)
                if fin:
                    store(i - 1)

            step(-1, True, False, False, 1)
            step(0, True, True, False, 0)
            with sp.Fori(0, (B - 2) // 2 - 1) as j:
                step(2 * j + 1, True, True, True, 1)
                step(2 * j + 2, True, True, True, 0)
            step(B - 3, True, True, True, 1)
            step(B - 2, True, True, True, 0, ahead=False)
            step(B - 1, False, True, True, 1)
            step(B, False, False, True, 0)
            sp.wait_ge(sem["out_written"], PER["out_written"] * B)

        @block.tensor
        def _(pe):
            mm = nc.tensor.matmul

            def prepare(a, fill, half):
                bank, (kind, k) = ps_a, fill
                pe.wait_ge(sem["a_drained"], upto("a_drained", a, a_nth[fill] - 1))
                if kind == "conv":
                    if k == 0:
                        pe.wait_ge(sem["x_loaded"], upto("x_loaded", a, 48))
                    g = 3 if k == NT - 1 else GR
                    r0 = GR * k
                    o = bank[0:g * G, 0:D]
                    for q, (dr, dc) in enumerate(((0, 0), (0, 1), (1, 0), (1, 1))):
                        last = mm(o, xa[:, dc, G * (r0 + dr):G * (r0 + dr + g)], w_conv[:, q],
                                  start=(q == 0), stop=False)
                    for dr in range(2):
                        last = mm(o, xb[:, G * (r0 + dr):G * (r0 + dr + g)], w_conv[:, 4 + dr],
                                  start=False, stop=(dr == 1))
                    last.then_inc(sem["a_filled"], 1)
                elif kind == "xnT":
                    if k == 0:
                        pe.wait_ge(sem["xn_ready"], upto("xn_ready", a, 1))
                    hf, tiles = quads[k]
                    for n, tile in enumerate(tiles):
                        last = nc.tensor.transpose(bank[0:96, n * TS:n * TS + rows(tile)],
                                                   xn[0:rows(tile), tile, 96 * hf:96 * hf + 96],
                                                   ident[0:rows(tile), 0:rows(tile)])
                    last.then_inc(sem["a_filled"], 1)
                elif kind == "qk":
                    c, hf = divmod(k, 2)
                    for kk in range(2):
                        last = mm(bank[0:96, 0:HF], w_qk[:, kk, 96 * c:96 * c + 96], xnT[0:96, kk, hf * HF:hf * HF + HF],
                                  start=(kk == 0), stop=(kk == 1))
                    last.then_inc(sem["a_filled"], 1)
                elif kind == "bound":
                    pe.wait_ge(sem["bound_chain"], upto("bound_chain", a, 2))
                    for c in range(2):
                        last = mm(bank[0:1, 6 * c:6 * c + 6], bound[:, c:c + 1], head_rows[:], start=True, stop=True,
                                  skip_group_check=True)
                    last.then_inc(sem["a_filled"], 1)
                else:
                    for n, tile in enumerate(pairs[k]):
                        for kk in range(2):
                            kp = 96 + kk
                            last = mm(bank[0:TL, n * D:n * D + D], xnT[0:kp, kk, TS * tile:TS * tile + TL],
                                      w_v[0:kp, kk], start=(kk == 0), stop=(kk == 1), skip_group_check=True)
                    last.then_inc(sem["a_filled"], 1)

            def finish(c, fill):
                bank, (kind, k) = ps_c, fill
                pe.wait_ge(sem["c_drained"], upto("c_drained", c, c_nth[fill] - 1))
                if kind == "proj":
                    if k == 0:
                        pe.wait_ge(sem["o_ready"], upto("o_ready", c, 3))
                    for n, tile in enumerate(pairs[k]):
                        for g in range(NG):
                            last = mm(bank[0:TL, n * D:n * D + D], oT[:, g, TS * tile:TS * tile + TL], w_p[:, g],
                                      start=(g == 0), stop=(g == NG - 1), skip_group_check=True)
                elif kind == "x2T":
                    if k == 0:
                        pe.wait_ge(sem["x2_ready"], upto("x2_ready", c, 1))
                    hf, tiles = quads[k]
                    for n, tile in enumerate(tiles):
                        last = nc.tensor.transpose(bank[0:96, n * TS:n * TS + rows(tile)],
                                                   x2[0:rows(tile), tile, 96 * hf:96 * hf + 96],
                                                   ident[0:rows(tile), 0:rows(tile)])
                elif kind == "lT":
                    hf = k
                    for kk in range(2):
                        last = mm(bank[0:NS, 0:HF], slots[:, kk], x2T[:, kk, hf * HF:hf * HF + HF],
                                  start=(kk == 0), stop=(kk == 1))
                elif kind == "logits":
                    for tile in range(NT):
                        for kk in range(2):
                            last = mm(bank[0:TL, tile * NS:tile * NS + NS], x2T[:, kk, TS * tile:TS * tile + TL],
                                      slots[:, kk], start=(kk == 0), stop=(kk == 1), skip_group_check=True)
                elif kind == "disp":
                    pe.wait_ge(sem["diag_ready"], upto("diag_ready", c, 1))
                    for tile in range(NT):
                        last = mm(bank[0:TL, tile * NS:tile * NS + NS], lT[:, TS * tile:TS * tile + TL], diag[:],
                                  start=True, stop=True, skip_group_check=True)
                elif kind == "cT":
                    pe.wait_ge(sem["comb_exp"], upto("comb_exp", c, 1))
                    for n, tile in enumerate(quads[k][1]):
                        last = nc.tensor.transpose(bank[0:NS, n * TS:n * TS + rows(tile)], lc[0:rows(tile), tile],
                                                   ident[0:rows(tile), 0:rows(tile)])
                elif kind == "xt":
                    for hf in range(2):
                        for tile in range(NT):
                            m = rows(tile)
                            last = mm(bank[0:96, hf * NS:hf * NS + NS], x2[0:m, tile, 96 * hf:96 * hf + 96],
                                      disp[0:m, tile], start=(tile == 0), stop=(tile == NT - 1), skip_group_check=True)
                elif kind == "hidden":
                    for m in range(2):
                        for kk in range(2):
                            last = mm(bank[0:96, m * NS:m * NS + NS], w_down[:, kk, 96 * m:96 * m + 96], xt[:, kk],
                                      start=(kk == 0), stop=(kk == 1), skip_group_check=True)
                elif kind == "yt":
                    pe.wait_ge(sem["hidden_ready"], upto("hidden_ready", c, 1))
                    for m in range(2):
                        last = mm(bank[0:NS, 0:D], hm[:, m], w_up[:, m], start=(m == 0), stop=(m == 1))
                else:
                    for n, tile in enumerate(pairs[k]):
                        last = mm(bank[0:TL, n * D:n * D + D], cT[:, TS * tile:TS * tile + TL], yt[:],
                                  start=True, stop=True, skip_group_check=True)
                last.then_inc(sem["c_filled"], 1)

            def scores(b, unit, heads, half):
                g, tile = divmod(unit, NT)
                for j in heads:
                    n = 4 * unit + j
                    pe.wait_ge(sem["exp_done"], upto("exp_done", b, n - 1))
                    if tile == 0 and j == 0:
                        pe.wait_ge(sem[f"group_loaded_{g}"], upto(f"group_loaded_{g}", b, 192))
                        pe.wait_ge(sem[f"shift_loaded_{g}"], upto(f"shift_loaded_{g}", b, 16))
                    for hf in range(2):
                        last = mm(ps_s[0:rows(tile), n % 2, hf, 0:HF], Ks[:, (half + g) % 2, j, TS * tile:TS * tile + rows(tile)],
                                  Qs[:, (half + g) % 2, j, hf * HF:hf * HF + HF], start=True, stop=True)
                    last.then_inc(sem["s_filled"], 1)

            def weigh(b, unit, half, hf):
                g, tile = divmod(unit, NT)
                m = rows(tile)
                if hf == 0:
                    pe.wait_ge(sem["exp_done"], upto("exp_done", b, 4 * unit + 4))
                    if unit == 0:
                        pe.wait_ge(sem["a_drained"], upto("a_drained", b, a_nth["v", 3]))
                if tile == 0:
                    pe.wait_ge(sem["o_bcast"], upto("o_bcast", b, 2 * g - 1 + hf))
                for j in range(4):
                    last = mm(ps_o[32 * j:32 * j + HD + 1, hf, 0:HF], v[0:m, half, tile, 4 * g + j],
                              probs[0:m, (half + unit) % 2, j, hf * HF:hf * HF + HF],
                              start=(tile == 0), stop=(tile == NT - 1), tile_position=(0, 32 * j))
                last.then_inc(sem["pv_done"], 1)

            def maxima(a, half):
                pe.wait_ge(sem["group_loaded_0"], upto("group_loaded_0", a, 192))
                for head in range(NH):
                    g, j = divmod(head, 4)
                    if j == 0 and g:
                        pe.wait_ge(sem["m_loaded"], upto("m_loaded", a, 192 * g))
                    at = half if g == 0 else 1 - half
                    for tile in range(NT):
                        n = head * NT + tile
                        if n >= 2:
                            pe.wait_ge(sem["m_drained"], upto("m_drained", a, n - 1))
                        else:
                            pe.wait_ge(sem["exp_done"], upto("exp_done", a - 1, 84))
                        for hf in range(2):
                            lo = hf * (HF - 1)
                            last = mm(ps_s[0:TL, n % 2, hf, 0:HF], Qs[0:KR, at, j, TS * tile:TS * tile + TL],
                                      Ks[0:KR, at, j, lo:lo + HF], start=True, stop=True)
                        last.then_inc(sem["m_filled"], 1)
                for n, tiles in enumerate(((0, 1, 2, 3), (4, 5, 6))):
                    pe.wait_ge(sem["m_drained"], upto("m_drained", a, 84))
                    for q, tile in enumerate(tiles):
                        last = nc.tensor.transpose(ps_s[0:NH, 0, n, q * TS:q * TS + rows(tile)],
                                                   mx[0:rows(tile), tile], ident[0:rows(tile), 0:rows(tile)])
                    last.then_inc(sem["m_filled"], 1)

            def step(i, prep, att, fin, parity):
                if att:
                    scores(i, 0, range(4), parity)
                for q in range(4 * UNITS):
                    unit, j = divmod(q, 4)
                    if att and unit + 1 < UNITS:
                        scores(i, unit + 1, (j,), parity)
                    if att and j in (1, 2):
                        weigh(i, unit, parity, j - 1)
                    if q in FILLS:
                        if FILLS[q][0] in PREPARES:
                            if prep:
                                prepare(i + 1, FILLS[q], 1 - parity)
                        elif fin:
                            finish(i - 1, FILLS[q])
                if prep:
                    pe.wait_ge(sem["flag_ready"], upto("flag_ready", i + 1, 1))
                    pe.sem_inc(sem["flag_seen"], 1)
                    with pe.If(pe.value_load(flag[0:1, 1 - parity:2 - parity]) > 0):
                        maxima(i + 1, 1 - parity)
                    with pe.Else():
                        pe.sem_inc(sem["m_filled"], PER["m_filled"])

            pe.wait_ge(setup_done, 1)
            step(-1, True, False, False, 1)
            step(0, True, True, False, 0)
            with pe.Fori(0, (B - 2) // 2) as j:
                step(2 * j + 1, True, True, True, 1)
                step(2 * j + 2, True, True, True, 0)
            step(B - 1, False, True, True, 1)
            step(B, False, False, True, 0)

        @block.scalar
        def _(act):
            def exps(b, unit, j, half):
                g, tile = divmod(unit, NT)
                m = rows(tile)
                n = 4 * unit + j
                act.wait_ge(sem["s_filled"], upto("s_filled", b, n + 1))
                if j == 0:
                    act.wait_ge(sem["pv_done"], upto("pv_done", b, 2 * (unit - 1)))
                nc.scalar.activation(probs[0:m, (half + unit) % 2, j].rearrange("p (a n) -> p a n", a=2),
                                     ps_s[0:m, n % 2, :, 0:HF], ACT.Exp).then_inc(sem["exp_done"], 1)

            def guess(b, g, part):
                if part == 0:
                    act.wait_ge(sem["o_bcast"], upto("o_bcast", b, 2 * g + 2))
                    nc.scalar.activation(rec[:], den[:], ACT.Ln).then_inc(sem["o_guess"], 1)
                else:
                    act.wait_ge(sem["o_guess"], upto("o_guess", b, 2 * g + 1))
                    nc.scalar.activation(rec[:], rec[:], ACT.Exp, scale=-1.0).then_inc(sem["o_guess"], 1)

            def copy_qk(a, k):
                c, hf = divmod(k, 2)
                act.wait_ge(sem["a_filled"], upto("a_filled", a, a_nth["qk", k]))
                if hf == 0:
                    act.wait_ge(sem["r_ready"], upto("r_ready", a, 2 * (c - 1)))
                nc.scalar.activation(f[:, c % 2, hf * HF:hf * HF + HF], ps_a[0:96, 0:HF], ACT.Identity,
                                     bias=b_qk[:, c:c + 1], scale=HD ** -0.5 if c < 2 else 1.0)\
                    .then_inc(sem["a_drained"], 1)

            def step(i, prep, att, fin, parity):
                for j in range(4):
                    if att:
                        exps(i, 0, j, parity)
                    if fin and j >= 2:
                        guess(i - 1, NG - 1, j - 2)
                for q in range(4 * UNITS):
                    unit, j = divmod(q, 4)
                    if att and unit + 1 < UNITS:
                        exps(i, unit + 1, j, parity)
                    if att and q in (4 * NT, 4 * NT + 1, 8 * NT, 8 * NT + 1):
                        guess(i, unit // NT - 1, j)
                    if prep and FILLS.get(q, ("", 0))[0] == "qk":
                        copy_qk(i + 1, FILLS[q][1])
                    if fin and q == AT["logits", 0] + 3:
                        act.wait_ge(sem["c_chain"], upto("c_chain", i - 1, 1))
                        nc.scalar.activation(lT[:, 0:N], lT[:, 0:N], ACT.Exp, bias=nmax[:], accum_out=dsum[:])\
                            .then_inc(sem["disp_exp"], 1)
                        act.wait_ge(sem["c_drained"], upto("c_drained", i - 1, c_nth["logits", 0]))
                        nc.scalar.activation(lc[:], lc[:], ACT.Exp).then_inc(sem["comb_exp"], 1)

            act.preload_act_table_set("natural_log_exp_and_others")
            act.wait_ge(setup_done, 1)
            step(-1, True, False, False, 1)
            step(0, True, True, False, 0)
            with act.Fori(0, (B - 2) // 2) as j:
                step(2 * j + 1, True, True, True, 1)
                step(2 * j + 2, True, True, True, 0)
            step(B - 1, False, True, True, 1)
            step(B, False, False, True, 0)

        @block.vector
        def _(dve):
            V = nc.vector
            made = [0]

            def link(ins):
                made[0] += 1
                ins.then_inc(setup_dve, 1)
                dve.wait_ge(setup_dve, made[0])

            V.memset(h[:].rearrange("p a t d -> p (a t d)"), 0.0)
            V.memset(xnT[0:96, :, N:NP], 0.0)
            V.memset(xnT[96:97], 1.0)
            V.memset(x2T[:, :, N:NP], 0.0)
            V.memset(Ks[KR:KS].rearrange("p a t d -> p (a t d)"), 1.0)
            V.memset(v[:, :, :, :, HD:HD + 1].rearrange("p a t g d -> p (a t g) d"), 1.0)
            V.memset(ps_o[:], 0.0)
            V.memset(neg[:], 0.0)
            V.memset(ve2[:, :, NT:8], 1.0)
            for n, value in enumerate((-0.5, 0.5, -1.0, LN_EPS, L2_EPS, float(D), 0.0)):
                last = V.memset(const[:, n], value)
            link(last)
            dve.wait_ge(params_loaded, 17 * 16)
            V.tensor_tensor(pos[:], pos[:], tokb[:].unsqueeze(1).to_broadcast([TG, NT, D]), ALU.add)
            V.tensor_tensor(cls[:, 0], cls[:, 0], cls[:, 1], ALU.add)
            V.tensor_scalar(b_qk[:, 0:2], b_qk[:, 0:2], HD ** -0.5, None, ALU.mult)
            link(V.tensor_tensor(sq[:], slots[:], slots[:], ALU.mult))
            link(V.tensor_reduce(nrm[:], sq[:].rearrange("p k (e s) -> p k s e", e=NEXP), axis=AX.X, op=ALU.add))
            dve.wait_ge(setup_pool, 1)
            link(V.tensor_scalar(nrm[:], nrm[:], L2_EPS, None, ALU.add))
            link(V.reciprocal(nrm[:], nrm[:]))
            link(V.tensor_scalar(nrm[:], nrm[:], scale_c[:], None, ALU.mult))
            for kk in range(2):
                last = V.tensor_tensor(slots[:, kk].rearrange("p (e s) -> p e s", e=NEXP),
                                       slots[:, kk].rearrange("p (e s) -> p e s", e=NEXP),
                                       nrm[:, kk].unsqueeze(1).to_broadcast([96, NEXP, SLOTS]), ALU.mult)
            last.then_inc(setup_done, 1)
            dve.wait_ge(cls_placed, 32)

            def prepare(a, fill, half):
                kind, k = fill
                if kind != "qk":
                    dve.wait_ge(sem["a_filled"], upto("a_filled", a, a_nth[fill]))
                if kind == "conv":
                    m = TGL if k == NT - 1 else TG
                    dve.wait_ge(sem["c_drained"], upto("c_drained", a - 2, c_nth["proj", k // 2]))
                    V.tensor_tensor(h[0:m, half, k], ps_a[0:m, 0:D], pos[0:m, k], ALU.add)\
                        .then_inc(sem["a_drained"], 1)
                elif kind == "xnT":
                    hf, tiles = quads[k]
                    c0 = TS * tiles[0]
                    c1 = TS * tiles[-1] + rows(tiles[-1])
                    V.tensor_copy(xnT[0:96, hf, c0:c1], ps_a[0:96, 0:c1 - c0]).then_inc(sem["a_drained"], 1)
                elif kind == "qk":
                    c, hf = divmod(k, 2)
                    cols = slice(hf * HF, hf * HF + HF)
                    dve.wait_ge(sem["a_drained"], upto("a_drained", a, a_nth[fill]))
                    dve.wait_ge(sem[f"parts_written_{c % 2}"], upto(f"parts_written_{c % 2}", a, 16 * (c // 2)))
                    V.tensor_copy(parts[:, c % 2, 0, cols], f[:, c % 2, cols]).then_inc(sem["hi_ready"], 1)
                    V.tensor_reduce(top[:, c, hf:hf + 1], f[:, c % 2, cols], axis=AX.X, op=ALU.max,
                                    apply_absolute_value=True)
                    dve.wait_ge(sem["hi_ready"], upto("hi_ready", a, k + 1))
                    V.tensor_tensor(r[:, c % 2, cols], f[:, c % 2, cols], parts[:, c % 2, 0, cols], ALU.subtract)\
                        .then_inc(sem["r_ready"], 1)
                elif kind == "bound":
                    V.tensor_reduce(most[:], ps_a[0:1, 0:12], axis=AX.X, op=ALU.max).then_inc(sem["a_drained"], 1)
                    dve.wait_ge(sem["a_drained"], upto("a_drained", a, a_nth[fill]))
                    dve.wait_ge(sem["flag_seen"], upto("flag_seen", a - 1, 0))
                    V.tensor_scalar(flag[0:1, half:half + 1], most[:], LIMIT, None, ALU.is_gt)\
                        .then_inc(sem["flag_ready"], 1)
                else:
                    n, t0 = len(pairs[k]), pairs[k][0]
                    V.tensor_copy(v[:, half, t0:t0 + n, :, 0:HD],
                                  ps_a[0:TL, 0:n * D].rearrange("p (t g d) -> p t g d", g=NH, d=HD))\
                        .then_inc(sem["a_drained"], 1)

            def bounds(a):
                dve.wait_ge(sem["r_ready"], upto("r_ready", a, 8))
                V.tensor_tensor(top[:, :, 0], top[:, :, 0], top[:, :, 1], ALU.max).then_inc(sem["bound_chain"], 1)
                dve.wait_ge(sem["bound_chain"], upto("bound_chain", a, 1))
                V.tensor_tensor(bound[:], top[:, 0:2, 0], top[:, 2:4, 0], ALU.mult).then_inc(sem["bound_chain"], 1)

            def carry(n):
                V.memset(held[:, n:n + 1], 0.0)

            def stats1(a, tile, half):
                dve.wait_ge(sem["a_drained"], upto("a_drained", a, a_nth["conv", tile]))
                if tile == 0:
                    dve.wait_ge(sem["txt_loaded"], upto("txt_loaded", a, 32))
                    carry(0)
                V.bn_stats(st[:, tile], h[:, half, tile]).then_inc(sem["stats_done"], 1)

            def stats2(c, k):
                dve.wait_ge(sem["c_drained"], upto("c_drained", c, c_nth["proj", k]))
                for tile in pairs[k]:
                    last = V.bn_stats(st2[:, tile], h2[:, tile])
                last.then_inc(sem["stats2_done"], 1)

            def combine(into, agg, done, chain, image, n):
                dve.wait_ge(sem[done], upto(done, image, PER[done]))
                carry(n)
                for tile in range(NT):
                    last = V.bn_aggr(agg[:, tile], into[:, tile])
                last.then_inc(sem[chain], 1)

            def factor2(c):
                dve.wait_ge(sem["ln2_pool"], upto("ln2_pool", c, 3))
                V.tensor_tensor(sc2[:, 0, 0:NT], pow2[:, 0, 0:NT], pow2[:, 1, 0:NT], ALU.mult)\
                    .then_inc(sem["ln2_chain"], 1)
                dve.wait_ge(sem["ln2_chain"], upto("ln2_chain", c, 2))
                V.tensor_scalar(sc2[:, 0, 0:NT], sc2[:, 0, 0:NT], L2_EPS, None, ALU.add).then_inc(sem["ln2_chain"], 1)
                dve.wait_ge(sem["ln2_chain"], upto("ln2_chain", c, 3))
                V.reciprocal(sc2[:, 0, 0:NT], sc2[:, 0, 0:NT]).then_inc(sem["ln2_chain"], 1)
                dve.wait_ge(sem["ln2_chain"], upto("ln2_chain", c, 4))
                V.tensor_tensor(sc2[:, 1, 0:NT], sc2[:, 0, 0:NT], pow2[:, 0, 0:NT], ALU.mult)\
                    .then_inc(sem["ln2_chain"], 1)
                dve.wait_ge(sem["ln2_chain"], upto("ln2_chain", c, 5))

            def normalise(dst, src, agg, factor, ready):
                for tile in range(NT):
                    last = V.tensor_scalar(dst[:, tile], src[:, tile], agg[:, tile, 0:1], factor[:, tile:tile + 1],
                                           ALU.subtract, ALU.mult)
                last.then_inc(sem[ready], 1)

            def maxima(a):
                for n in range(TILES):
                    head, tile = divmod(n, NT)
                    dve.wait_ge(sem["m_filled"], upto("m_filled", a, n + 1))
                    V.tensor_reduce(mx[:, tile, head:head + 1], ps_s[0:TL, n % 2, :, 0:HF], axis=AX.XY, op=ALU.max)\
                        .then_inc(sem["m_drained"], 1)
                dve.wait_ge(sem["shift_written"], upto("shift_written", a, 0))
                dve.wait_ge(sem["m_filled"], upto("m_filled", a, 86))
                V.tensor_scalar(neg[:, 0:4 * TS], ps_s[0:NH, 0, 0, 0:4 * TS], -1.0, None, ALU.mult)
                V.tensor_scalar(neg[:, 4 * TS:N], ps_s[0:NH, 0, 1, 0:N - 4 * TS], -1.0, None, ALU.mult)\
                    .then_inc(sem["m_chain"], 1)
                dve.wait_ge(sem["m_chain"], upto("m_chain", a, 1))
                V.tensor_copy(shift[:, 0], neg[:]).then_inc(sem["m_chain"], 1)
                dve.wait_ge(sem["m_chain"], upto("m_chain", a, 2))
                V.tensor_tensor(shift[:, 1], neg[:], shift[:, 0], ALU.subtract).then_inc(sem["shift_ready"], 1)

            def collect(b, g, hf):
                cols = slice(hf * HF, hf * HF + HF)
                dve.wait_ge(sem["pv_done"], upto("pv_done", b, 2 * NT * (g + 1) - 1 + hf))
                dve.wait_ge(sem["c_filled"], upto("c_filled", b - 1, c_nth["proj", 3]))
                V.tensor_copy(oT[:, g, cols], ps_o[:, hf, 0:HF]).then_inc(sem["o_copied"], 1)
                if hf == 0:
                    dve.wait_ge(sem["o_ready"], upto("o_ready", b, g))
                    carry(2)
                V.stream_shuffle(den[:, cols], ps_o[:, hf, 0:HF], [HD] * 32).then_inc(sem["o_bcast"], 1)

            def divide(b, g, part):
                if part == 0:
                    dve.wait_ge(sem["o_guess"], upto("o_guess", b, 2 * g + 2))
                    V.tensor_tensor(den[:], den[:], rec[:], ALU.mult).then_inc(sem["o_chain"], 1)
                elif part == 1:
                    dve.wait_ge(sem["o_chain"], upto("o_chain", b, 2 * g + 1))
                    V.scalar_tensor_tensor(den[:], den[:], 2.0, rec[:], ALU.subtract, ALU.mult)\
                        .then_inc(sem["o_chain"], 1)
                else:
                    dve.wait_ge(sem["o_chain"], upto("o_chain", b, 2 * g + 2))
                    V.scalar_tensor_tensor(oT[:, g], oT[:, g], -1.0, den[:], ALU.mult, ALU.mult)\
                        .then_inc(sem["o_ready"], 1)

            step_count = [0]

            def chain(ins, c):
                step_count[0] += 1
                ins.then_inc(sem["c_chain"], 1)
                dve.wait_ge(sem["c_chain"], upto("c_chain", c, step_count[0]))

            def finish(c, fill, half):
                kind, k = fill
                dve.wait_ge(sem["c_filled"], upto("c_filled", c, c_nth[fill]))
                drained = lambda ins: ins.then_inc(sem["c_drained"], 1)
                if kind == "proj":
                    n, t0 = len(pairs[k]), pairs[k][0]
                    drained(V.tensor_tensor(h2[:, t0:t0 + n], ps_c[0:TL, 0:n * D].rearrange("p (t d) -> p t d", d=D),
                                            h[:, half, t0:t0 + n], ALU.add))
                elif kind == "x2T":
                    hf, tiles = quads[k]
                    c0 = TS * tiles[0]
                    c1 = TS * tiles[-1] + rows(tiles[-1])
                    drained(V.tensor_copy(x2T[:, hf, c0:c1], ps_c[0:96, 0:c1 - c0]))
                elif kind == "lT":
                    c0, c1 = (0, HF) if k == 0 else (HF, N)
                    drained(V.tensor_copy(lT[:, c0:c1], ps_c[0:NS, 0:c1 - c0]))
                    if k == 1:
                        dve.wait_ge(sem["c_drained"], upto("c_drained", c, c_nth[fill]))
                        chain(V.tensor_reduce(nmax[:], lT[:, 0:N], axis=AX.X, op=ALU.max, negate=True), c)
                elif kind == "logits":
                    logits = ps_c[0:TL, 0:NT * NS].rearrange("p (t s) -> p t s", s=NS)
                    chain(V.tensor_reduce(cmax[:], logits, axis=AX.X, op=ALU.max), c)
                    drained(V.tensor_tensor(lc[:], logits, cmax[:].unsqueeze(2).to_broadcast([TL, NT, NS]),
                                            ALU.subtract))
                elif kind == "disp":
                    drained(V.tensor_copy(disp[:].rearrange("p t s -> p (t s)"), ps_c[0:TL, 0:NT * NS]))
                elif kind == "cT":
                    tiles = quads[k][1]
                    c0 = TS * tiles[0]
                    c1 = TS * tiles[-1] + rows(tiles[-1])
                    drained(V.tensor_copy(cT[:, c0:c1], ps_c[0:NS, 0:c1 - c0]))
                elif kind == "xt":
                    drained(V.tensor_copy(xt[:].rearrange("p a s -> p (a s)"), ps_c[0:96, 0:2 * NS]))
                elif kind == "hidden":
                    drained(V.tensor_tensor(u[:], ps_c[0:96, 0:2 * NS].rearrange("p (a s) -> p a s", s=NS),
                                            b_down[:].unsqueeze(2).to_broadcast([96, 2, NS]), ALU.add))
                    dve.wait_ge(sem["c_drained"], upto("c_drained", c, c_nth[fill]))
                elif kind == "yt":
                    drained(V.tensor_tensor(yt[:], ps_c[0:NS, 0:D], b_up[:], ALU.add))
                else:
                    if k == 0:
                        dve.wait_ge(sem["out_written"], upto("out_written", c, 0))
                    for n, tile in enumerate(pairs[k]):
                        last = V.scalar_tensor_tensor(y[:, tile], ps_c[0:TL, n * D:n * D + D], crec[:, tile:tile + 1],
                                                      h2[:, tile], ALU.mult, ALU.add)
                    drained(last)

            def weights(c):
                dve.wait_ge(sem["disp_exp"], upto("disp_exp", c, 1))
                chain(V.reciprocal(drec[:], dsum[:]), c)
                V.tensor_scalar(diag[:], ident[0:NS, 0:NS], drec[:], None, ALU.mult).then_inc(sem["diag_ready"], 1)
                dve.wait_ge(sem["comb_exp"], upto("comb_exp", c, 1))
                chain(V.tensor_reduce(csum[:], lc[:], axis=AX.X, op=ALU.add), c)
                chain(V.reciprocal(crec[:], csum[:]), c)

            def gelu(c, part):
                if part == 0:
                    chain(V.tensor_scalar(uc[:], u[:], 0.5 ** 0.5, ERF_MAX, ALU.mult, ALU.min), c)
                    chain(V.tensor_scalar(uc[:], uc[:], -ERF_MAX, None, ALU.max), c)
                    chain(V.tensor_tensor(u2[:], uc[:], uc[:], ALU.mult), c)
                elif part == 1:
                    chain(V.tensor_scalar(pn[:], u2[:], ERF_NUM[0], None, ALU.mult), c)
                    for coef in ERF_NUM[1:-1]:
                        chain(V.scalar_tensor_tensor(pn[:], pn[:], coef, u2[:], ALU.add, ALU.mult), c)
                    chain(V.scalar_tensor_tensor(pn[:], pn[:], ERF_NUM[-1], uc[:], ALU.add, ALU.mult), c)
                elif part == 2:
                    chain(V.tensor_scalar(pd[:], u2[:], ERF_DEN[0], None, ALU.mult), c)
                    for coef in ERF_DEN[1:-1]:
                        chain(V.scalar_tensor_tensor(pd[:], pd[:], coef, u2[:], ALU.add, ALU.mult), c)
                else:
                    chain(V.tensor_scalar(pd[:], pd[:], ERF_DEN[-1], None, ALU.add), c)
                    chain(V.reciprocal(pd[:], pd[:]), c)
                    chain(V.tensor_tensor(pn[:], pn[:], pd[:], ALU.mult), c)
                    chain(V.scalar_tensor_tensor(pn[:], pn[:], 1.0, u[:], ALU.add, ALU.mult), c)
                    V.scalar_tensor_tensor(hm[:], pn[:], 0.5, mask[:], ALU.mult, ALU.mult)\
                        .then_inc(sem["hidden_ready"], 1)

            DIVIDE = {0: 4 * NT + 2, 1: 8 * NT + 2}
            COMBINE1, NORM1 = AT["conv", NT - 1], AT["conv", NT - 1] + 3
            COMBINE2, NORM2 = AT["proj", 3], AT["proj", 3] + 3
            WEIGHTS, GELU, BOUNDS = AT["logits", 0] + 5, AT["hidden", 0] + 1, AT["bound", 0] - 3

            def step(i, prep, att, fin, parity):
                step_count[0] = 0
                if fin:
                    for part in range(3):
                        divide(i - 1, NG - 1, part)
                for q in range(4 * UNITS):
                    unit, j = divmod(q, 4)
                    if att and unit % NT == NT - 1 and j in (1, 2):
                        collect(i, unit // NT, j - 1)
                    if q in FILLS:
                        if FILLS[q][0] in PREPARES:
                            if prep:
                                prepare(i + 1, FILLS[q], 1 - parity)
                        elif fin:
                            finish(i - 1, FILLS[q], 1 - parity)
                    if prep and q >= AT["proj", 3]:
                        for tile in range(NT):
                            if q == max(AT["conv", tile], AT["proj", 3] + 1 + tile // 2):
                                stats1(i + 1, tile, 1 - parity)
                    if fin and FILLS.get(q, ("", 0))[0] == "proj":
                        stats2(i - 1, FILLS[q][1])
                    if fin and q == COMBINE2:
                        combine(st2, mv2, "stats2_done", "ln2_chain", i - 1, 1)
                    if fin and q == NORM2:
                        factor2(i - 1)
                        normalise(x2, h2, mv2, sc2[:, 1], "x2_ready")
                    if prep and q == COMBINE1:
                        combine(st, mv, "stats_done", "a_chain", i + 1, 0)
                    if prep and q == NORM1:
                        dve.wait_ge(sem["ln1_pool"], upto("ln1_pool", i + 1, 2))
                        normalise(xn, h[:, 1 - parity], mv, rstd, "xn_ready")
                    for g in DIVIDE:
                        if att and q - DIVIDE[g] in (0, 1, 2):
                            divide(i, g, q - DIVIDE[g])
                    if fin and q == WEIGHTS:
                        weights(i - 1)
                    if fin and q - GELU in (0, 1, 2, 3):
                        gelu(i - 1, q - GELU)
                    if prep and q == BOUNDS:
                        bounds(i + 1)
                if fin:
                    assert step_count[0] == PER["c_chain"], step_count
                if prep:
                    dve.wait_ge(sem["flag_ready"], upto("flag_ready", i + 1, 1))
                    dve.sem_inc(sem["flag_seen"], 1)
                    with dve.If(dve.value_load(flag[0:1, 1 - parity:2 - parity]) > 0):
                        maxima(i + 1)
                    with dve.Else():
                        dve.sem_inc(sem["m_drained"], PER["m_drained"])
                        dve.sem_inc(sem["m_chain"], PER["m_chain"])
                        dve.sem_inc(sem["shift_ready"], PER["shift_ready"])

            step(-1, True, False, False, 1)
            step(0, True, True, False, 0)
            with dve.Fori(0, (B - 2) // 2) as j:
                step(2 * j + 1, True, True, True, 1)
                step(2 * j + 2, True, True, True, 0)
            step(B - 1, False, True, True, 1)
            step(B, False, False, True, 0)

        @block.gpsimd
        def _(pool):
            G_ = nc.gpsimd
            pool.wait_ge(setup_dve, 3)
            G_.tensor_tensor(nrm[:].rearrange("p a s -> p (a s)"), nrm[:].rearrange("p a s -> p (a s)"),
                             const[0:96, 1, 0:2 * SLOTS], ALU.pow).then_inc(setup_pool, 1)

            def layernorm1(a):
                pool.wait_ge(sem["a_chain"], upto("a_chain", a, 1))
                G_.tensor_tensor(ve[:, 0:NT], mv[:, :, 1], const[0:TL, 3, 0:NT], ALU.add).then_inc(sem["ln1_pool"], 1)
                pool.wait_ge(sem["ln1_pool"], upto("ln1_pool", a, 1))
                G_.tensor_tensor(rstd[:, 0:NT], ve[:, 0:NT], const[0:TL, 0, 0:NT], ALU.pow).then_inc(sem["ln1_pool"], 1)

            def layernorm2(c):
                pool.wait_ge(sem["ln2_chain"], upto("ln2_chain", c, 1))
                G_.tensor_tensor(ve2[:, 0, 0:NT], mv2[:, :, 1], const[0:TL, 3, 0:NT], ALU.add)\
                    .then_inc(sem["ln2_pool"], 1)
                G_.tensor_tensor(ve2[:, 1, 0:NT], mv2[:, :, 1], const[0:TL, 5, 0:NT], ALU.mult)\
                    .then_inc(sem["ln2_pool"], 1)
                pool.wait_ge(sem["ln2_pool"], upto("ln2_pool", c, 2))
                G_.tensor_tensor(pow2[:], ve2[:], const[0:TL, 0:2], ALU.pow).then_inc(sem["ln2_pool"], 1)

            def split(a, c):
                pool.wait_ge(sem["r_ready"], upto("r_ready", a, 2 * c + 2))
                G_.tensor_tensor(parts[:, c % 2, 1], r[:, c % 2], const[0:96, 6, 0:1].to_broadcast([96, NP]), ALU.add).then_inc(sem["mid_ready"], 1)
                pool.wait_ge(sem["mid_ready"], upto("mid_ready", a, c + 1))
                G_.tensor_tensor(parts[:, c % 2, 2], r[:, c % 2], parts[:, c % 2, 1], ALU.subtract)\
                    .then_inc(sem["parts_ready"], 1)

            def step(i, prep, att, fin, parity):
                if fin:
                    layernorm2(i - 1)
                if prep:
                    layernorm1(i + 1)
                    for c in range(4):
                        split(i + 1, c)

            step(-1, True, False, False, 1)
            step(0, True, True, False, 0)
            with pool.Fori(0, (B - 2) // 2) as j:
                step(2 * j + 1, True, True, True, 1)
                step(2 * j + 2, True, True, True, 0)
            step(B - 1, False, True, True, 1)
            step(B, False, False, True, 0)


def kernel(**inputs):
    import numpy as np
    import concourse.bacc as bacc
    from concourse.bass_utils import run_bass_kernel_spmd

    inp = {k: np.asarray(v) for k, v in inputs.items()}
    f32, bf16 = np.float32, mybir.dt.np(BF16)
    B = inp["x"].shape[0]
    blocks = inp["x"].reshape(B, C, BG, S, BG, S).transpose(0, 1, 3, 5, 2, 4).reshape(B, C * S * S, BG, BG)
    x = np.stack([blocks[..., :G], blocks[..., 1:]], axis=1).reshape(B, 2, C * S * S, BG * G)
    w = inp["L0_tok_w"].reshape(D, C, 2, S, 2, S).transpose(2, 4, 1, 3, 5, 0).reshape(2, 2, C * S * S, D)
    w_conv = np.stack([w[0, 0, :128], w[0, 1, :128], w[1, 0, :128], w[1, 1, :128],
                       np.concatenate([w[0, 0, 128:], w[0, 1, 128:]]),
                       np.concatenate([w[1, 0, 128:], w[1, 1, 128:]])], axis=1)
    qkv = inp["L0_attn_qkv_w"].T.reshape(2, 96, 3 * D).transpose(1, 0, 2)
    qkv_b = inp["L0_attn_qkv_b"]
    w_v = np.zeros((97, 2, D), f32)
    w_v[:96] = qkv[:, :, 2 * D:]
    w_v[96, 1] = qkv_b[2 * D:]
    w_p = np.zeros((NG, 4, 32, D), f32)
    w_p[:, :, :HD] = inp["L0_attn_proj_w"].T.reshape(NG, 4, HD, D)
    w_p[0, 0, HD] = inp["L0_attn_proj_b"]
    position = inp["L0_tok_pos_embedding"][0]
    pos = np.zeros((TG, NT, D), f32)
    pos[:, :NT - 1] = position[1:1 + TG * (NT - 1)].reshape(NT - 1, TG, D).transpose(1, 0, 2)
    pos[:TGL, NT - 1] = position[1 + TG * (NT - 1):]
    halves = lambda a: a.reshape(2, 96, -1).transpose(1, 0, 2)
    expert = np.arange(NEXP * HID) // HID
    arrays = {
        "x": x, "txt": inp["txt"], "w_conv": w_conv,
        "w_qk": qkv[:, :, :2 * D], "b_qk": qkv_b[:2 * D].reshape(4, 96).T, "w_v": w_v,
        "w_p": w_p.reshape(NG, 128, D).transpose(1, 0, 2), "pos": pos, "tok_b": inp["L0_tok_b"],
        "cls": np.concatenate([inp["L0_tok_cls_token"].reshape(1, 1, D), position[:1][None]], axis=1),
        "slots": halves(inp["L0_ffn_slot_params"].reshape(D, NS)),
        "slot_scale": inp["L0_ffn_scale"].reshape(1),
        "w_down": halves(inp["L0_ffn_W_down"].transpose(1, 0, 2).reshape(D, D)),
        "b_down": inp["L0_ffn_b_down"].reshape(2, 96).T,
        "w_up": halves(inp["L0_ffn_W_up"].reshape(D, D)),
        "b_up": np.repeat(inp["L0_ffn_b_up"], SLOTS, axis=0),
        "head_rows": np.repeat(np.eye(6, dtype=f32), HD, axis=0), "no_shift": np.zeros((2, NH, NP), bf16),
        "ident": np.eye(128, dtype=f32),
        "expert_mask": halves((expert[:, None] == np.arange(NS)[None] // SLOTS).astype(f32)),
    }
    arrays = {f"in_{k}": np.ascontiguousarray(v) for k, v in arrays.items()}
    nc = bacc.Bacc("TRN2", target_bir_lowering=False, num_devices=1)
    nc.disable_value_cache = True
    t = {k[3:]: nc.dram_tensor(k, v.shape, mybir.dt.from_np(v.dtype), kind="ExternalInput").ap()
         for k, v in arrays.items()}
    scr_parts = nc.dram_tensor("scr_parts", [4, 96, 3, NP], BF16, kind="Internal").ap()
    scr_shift = nc.dram_tensor("scr_shift", [2, NH, NP], BF16, kind="Internal").ap()
    out = nc.dram_tensor("out", [B, N, D], F32, kind="ExternalOutput").ap()
    early_fusion(nc, B, t, scr_parts, scr_shift, out)
    got = run_bass_kernel_spmd(nc, [arrays], core_ids=[0])
    return got.results[0]["out"]
```

```python
from contextlib import ExitStack

import concourse.bass as bass
from concourse import mybir

ALU = mybir.AluOpType
ACT = mybir.ActivationFunctionType
AX = mybir.AxisListType
F32 = mybir.dt.float32
BF16 = mybir.dt.bfloat16

C, IMG, P, S, D = 3, 224, 16, 8, 192
G = (IMG - P) // S + 1
BG = IMG // S
TXT = 77
NH, HD = 12, 16
NEXP, SLOTS, HID = 8, 4, 24
NS = NEXP * SLOTS
N = G * G + 1 + TXT
NT = 7
GR = 4
TG = GR * G
TGL = G * G - (NT - 1) * TG
TX = 7
TS = TG + TX
TL = N - (NT - 1) * TS
NP = N + 1
HF = NP // 2
KB = 6
KR = KB * HD
KS = KR + 2
NG = NH // 4
UNITS = NG * NT
TILES = UNITS * 4
Q_PARTS = (0, 0, 1, 1, 0, 2)
K_PARTS = (0, 1, 0, 1, 2, 0)
LN_EPS, L2_EPS = 1e-5, 1e-6
LIMIT = 36.0
ERF_NUM = (0.00022905065861350646, 0.0034082910107109506, 0.050955695062380861, 0.18520832239976145,
           1.128379143519084)
ERF_DEN = (-1.1791602954361697e-7, 0.000023547966471313185, 0.0010179625278914885, 0.014070470171167667,
           0.11098505178285362, 0.49746925110067538, 1.0)
ERF_MAX = 3.7439211627767994

PER = dict(
    x_loaded=48, txt_loaded=32, a_filled=22, a_drained=22, stats_done=7, a_chain=1, bound_chain=4, flag_ready=1,
    flag_seen=3, ln1_pool=2, xn_ready=1,
    hi_ready=6, r_ready=6, mid_ready=3, parts_ready=3, parts_written_0=16, parts_written_1=16, parts_written_2=16,
    group_loaded_0=192, group_loaded_1=192, group_loaded_2=192, m_loaded=384, shift_written=16,
    shift_loaded_0=16, shift_loaded_1=16, shift_loaded_2=16, s_filled=84, exp_done=84, pv_done=42,
    o_copied=6, o_bcast=6, o_guess=6, o_chain=7, o_ready=3,
    m_filled=86, m_drained=84, m_chain=2, shift_ready=1,
    c_filled=23, c_drained=23, c_chain=23, stats2_done=4, ln2_chain=5, ln2_pool=3, x2_ready=1,
    disp_exp=1, combine_ready=1, comb_exp=1, diag_ready=1,
    hidden_ready=1, out_written=80,
)
START = dict(c_drained=1, out_written=1)


def early_fusion(nc, B, t, scr_parts, scr_shift, out):
    with ExitStack() as ctx:
        def sb(name, shape, dt=F32):
            return ctx.enter_context(nc.sbuf_tensor(name, shape, dt))

        sem = {name: ctx.enter_context(nc.semaphore(name)) for name in PER}
        w_conv_loaded = ctx.enter_context(nc.semaphore("w_conv_loaded"))
        params_loaded = ctx.enter_context(nc.semaphore("params_loaded"))
        cls_placed = ctx.enter_context(nc.semaphore("cls_placed"))
        setup_dve = ctx.enter_context(nc.semaphore("setup_dve"))
        setup_pool = ctx.enter_context(nc.semaphore("setup_pool"))
        setup_done = ctx.enter_context(nc.semaphore("setup_done"))

        w_conv = sb("w_conv_sb", [128, 6, D])
        w_qk = sb("w_qk_sb", [96, 2, 2 * D])
        b_qk = sb("b_qk_sb", [128, 3])
        w_v = sb("w_v_sb", [97, 2, D])
        w_p = sb("w_p_sb", [128, 2, D])
        minus_first = sb("minus_first_sb", [128, 1])
        minus_last = sb("minus_last_sb", [128, 1])
        pos = sb("pos_sb", [TG, NT, D])
        slots = sb("slots_sb", [96, 2, NS])
        w_down = sb("w_down_sb", [96, 2, D])
        b_down = sb("b_down_sb", [96, 2])
        w_up = sb("w_up_sb", [96, 2, D])
        b_up = sb("b_up_sb", [NS, D])
        ident = sb("ident_sb", [128, 128])
        mask = sb("mask_sb", [96, 2, NS])
        cls = sb("cls_sb", [1, 2, D])
        tokb = sb("tokb_sb", [TG, D])
        scale_c = sb("scale_c", [96, 1])
        sq = sb("sq", [96, 2, NS])
        nrm = sb("nrm", [96, 2, SLOTS])
        const = sb("const", [128, 7, 8])
        held = sb("held", [1, 8])

        xa = sb("xa_sb", [128, 2, BG * G])
        xb = sb("xb_sb", [128, BG * G])
        h = sb("h", [TL, 2, NT, D])
        xn = sb("xn", [TL, NT, D])
        xnT = sb("xnT", [97, 2, NP])
        st = sb("st", [TL, NT, 6])
        mv = sb("mv", [TL, NT, 2])
        ve = sb("ve", [TL, 8])
        rstd = sb("rstd", [TL, 8])
        f = sb("f", [128, 2, NP])
        r = sb("r", [128, 2, NP])
        parts = sb("parts", [128, 2, 3, NP], BF16)
        Qs = sb("Qs", [KS, 2, 4, NP], BF16)
        Ks = sb("Ks", [KS, 2, 4, NP], BF16)
        v = sb("v", [TL, 2, NT, NH, HD + 1])
        top = sb("top", [128, 3, 2])
        bound = sb("bound", [1, 2 * D])
        head_bound = sb("head_bound", [1, NH])
        most = sb("most", [1, 1])
        flag = sb("flag", [1, 2], mybir.dt.int32)
        mx = sb("mx", [TL, NT, NH])
        neg = sb("neg", [NH, NP])
        shift = sb("shift", [NH, 2, NP], BF16)
        probs = sb("probs", [TL, 2, 4, NP])
        den = sb("den", [128, NP])
        rec = sb("rec", [128, NP])
        oT = sb("oT", [128, NG, NP])
        h2 = sb("h2", [TL, NT, D])
        x2 = sb("x2", [TL, NT, D])
        x2T = sb("x2T", [96, 2, NP])
        st2 = sb("st2", [TL, NT, 6])
        mv2 = sb("mv2", [TL, NT, 2])
        ve2 = sb("ve2", [TL, 2, 8])
        pow2 = sb("pow2", [TL, 2, 8])
        sc2 = sb("sc2", [TL, 2, 8])
        lT = sb("lT", [NS, NP])
        nmax = sb("nmax", [NS, 1])
        dsum = sb("dsum", [NS, 1])
        drec = sb("drec", [NS, 1])
        diag = sb("diag", [NS, NS])
        lc = sb("lc", [TL, NT, NS])
        cmax = sb("cmax", [TL, NT])
        csum = sb("csum", [TL, NT])
        crec = sb("crec", [TL, NT])
        disp = sb("disp", [TL, NT, NS])
        cT = sb("cT", [NS, NP])
        xt = sb("xt", [96, 2, NS])
        u = sb("u", [96, 2, NS])
        uc = sb("uc", [96, 2, NS])
        u2 = sb("u2", [96, 2, NS])
        pn = sb("pn", [96, 2, NS])
        pd = sb("pd", [96, 2, NS])
        hm = sb("hm", [96, 2, NS])
        yt = sb("yt", [NS, D])
        y = sb("y", [TL, NT, D])

        ps_s = ctx.enter_context(nc.psum_tensor("ps_s", [128, 2, 2, 512], F32))
        ps_o = ctx.enter_context(nc.psum_tensor("ps_o", [128, 2, 512], F32))
        ps_a = ctx.enter_context(nc.psum_tensor("ps_a", [128, 512], F32))
        ps_c = ctx.enter_context(nc.psum_tensor("ps_c", [128, 512], F32))

        def upto(name, image, count):
            value = image * PER[name] + count + START.get(name, 0)
            return max(value, 0) if isinstance(value, int) else value

        def rows(tile):
            return TL if tile == NT - 1 else TS

        FILLS = {3: ("conv", 0), 6: ("proj", 0), 8: ("proj", 1), 9: ("conv", 1), 10: ("conv", 2), 11: ("proj", 2),
                 12: ("conv", 3), 15: ("proj", 3), 16: ("conv", 4), 17: ("conv", 5), 20: ("conv", 6),
                 21: ("x2T", 0), 22: ("x2T", 1), 23: ("x2T", 2), 25: ("x2T", 3), 27: ("logits", 0), 28: ("xnT", 0),
                 29: ("logits", 1), 30: ("xnT", 1), 31: ("lT", 0), 32: ("xnT", 2), 33: ("lT", 1), 34: ("xnT", 3),
                 36: ("qk", 0), 39: ("qk", 1), 42: ("qk", 2), 43: ("disp", 0), 45: ("qk", 3), 46: ("xt", 0),
                 47: ("xt", 1), 49: ("qk", 4), 51: ("hidden", 0), 52: ("qk", 5), 53: ("cT", 0), 56: ("v", 0),
                 59: ("cT", 1), 60: ("v", 1), 63: ("yt", 0), 64: ("bound", 0), 67: ("y", 0), 71: ("v", 2),
                 72: ("y", 1), 76: ("y", 2), 79: ("v", 3), 83: ("y", 3)}
        PREPARES = ("conv", "xnT", "qk", "v", "bound")
        AT = {fill: quarter for quarter, fill in FILLS.items()}
        a_order = [FILLS[q] for q in sorted(FILLS) if FILLS[q][0] in PREPARES]
        c_order = [FILLS[q] for q in sorted(FILLS) if FILLS[q][0] not in PREPARES]
        a_nth = {fill: n + 1 for n, fill in enumerate(a_order)}
        c_nth = {fill: n + 1 for n, fill in enumerate(c_order)}
        assert len(a_order) == PER["a_filled"] and len(c_order) == PER["c_filled"]
        pairs = [(0, 1), (2, 3), (4, 5), (6,)]
        quads = [(half, ts) for half in range(2) for ts in ((0, 1, 2, 3), (4, 5, 6))]

        block = ctx.enter_context(nc.Block())

        @block.sync
        def _(sp):
            def load_x(a):
                sp.wait_ge(sem["a_filled"], upto("a_filled", a - 1, a_nth["conv", NT - 1]))
                src = t["x"][bass.ds(a, 1)].rearrange("a s p n -> p (a s) n")
                sp.dma_start(xa[:], src[0:128]).then_inc(sem["x_loaded"], 16)
                sp.dma_start(xb[0:64], src[128:192, 0]).then_inc(sem["x_loaded"], 16)
                sp.dma_start(xb[64:128], src[128:192, 1]).then_inc(sem["x_loaded"], 16)

            load_x(0)
            sp.dma_start(w_conv[:], t["w_conv"]).then_inc(w_conv_loaded, 16)
            load = lambda dst, src: sp.dma_start(dst, src).then_inc(params_loaded, 16)
            load(w_qk[:], t["w_qk"])
            load(b_qk[:], t["b_qk"])
            load(w_v[:], t["w_v"])
            load(pos[:], t["pos"])
            load(tokb[:], t["tok_b"].partition_broadcast(TG))
            load(cls[:, :, :], t["cls"])
            load(ident[:], t["ident"])
            load(w_p[:], t["w_p"])
            load(slots[:], t["slots"])
            load(scale_c[:], t["slot_scale"].partition_broadcast(96))
            load(w_down[:], t["w_down"])
            load(b_down[:], t["b_down"])
            load(w_up[:], t["w_up"])
            load(b_up[:], t["b_up"])
            load(mask[:], t["expert_mask"])
            load(minus_first[:], t["minus_first"])
            load(minus_last[:], t["minus_last"])

            def load_txt(a, half):
                if not isinstance(a, int) or a >= 2:
                    sp.wait_ge(sem["c_drained"], upto("c_drained", a - 2, c_nth["proj", 3]))
                src = t["txt"][bass.ds(a, 1)].rearrange("a n d -> (a n) d")
                sp.dma_start(h[TG:TS, half, 0:NT - 1, :],
                             src[0:TX * (NT - 1)].rearrange("(t r) d -> r t d", r=TX)).then_inc(sem["txt_loaded"], 16)
                sp.dma_start(h[TGL + 1:TL, half, NT - 1, :], src[TX * (NT - 1):]).then_inc(sem["txt_loaded"], 16)

            def write_parts(a, half):
                for c in range(3):
                    if c == 0:
                        sp.wait_ge(sem["group_loaded_2"], upto("group_loaded_2", a, 0))
                    sp.wait_ge(sem["parts_ready"], upto("parts_ready", a, c + 1))
                    sp.dma_start(scr_parts[128 * c:128 * c + 128], parts[:, (half + c) % 2])\
                        .then_inc(sem[f"parts_written_{c}"], 16)

            def load_group(g, half, signal):
                for first, dst, which in ((0, Qs, Q_PARTS), (D, Ks, K_PARTS)):
                    src = scr_parts[first:first + D].rearrange("(h d) s n -> d h s n", d=HD)
                    for b, part in enumerate(which):
                        sp.dma_start(dst[HD * b:HD * b + HD, half], src[:, 4 * g:4 * g + 4, part])\
                            .then_inc(sem[signal], 16)

            def load_shift(g, half):
                sp.dma_start(Qs[KR:KS, half], scr_shift[:, 4 * g:4 * g + 4])\
                    .then_inc(sem[f"shift_loaded_{g}"], 16)

            def load_for_maxima(a, half):
                for g in (1, 2):
                    if g == 1:
                        sp.wait_ge(sem["s_filled"], upto("s_filled", a, 0))
                    else:
                        sp.wait_ge(sem["m_filled"], upto("m_filled", a, 56))
                    load_group(g, half, "m_loaded")

            def send_shift(a, half):
                sp.wait_ge(sem["shift_ready"], upto("shift_ready", a, 1))
                sp.dma_start(scr_shift.rearrange("s h n -> h s n"), shift[:]).then_inc(sem["shift_written"], 16)
                sp.wait_ge(sem["shift_written"], upto("shift_written", a, 16))
                load_shift(0, half)

            def store(c):
                dst = out[bass.ds(c, 1)].rearrange("a n d -> (a n) d")
                sp.wait_ge(sem["c_drained"], upto("c_drained", c, c_nth["y", 3]))
                put = lambda d, s: sp.dma_start(d, s).then_inc(sem["out_written"], 16)
                put(dst[1:1 + TG * (NT - 1)].rearrange("(t p) d -> p t d", p=TG), y[0:TG, 0:NT - 1])
                put(dst[1 + TG * (NT - 1):1 + G * G], y[0:TGL, NT - 1])
                put(dst[0:1], y[TGL:TGL + 1, NT - 1])
                put(dst[1 + G * G:1 + G * G + TX * (NT - 1)].rearrange("(t r) d -> r t d", r=TX), y[TG:TS, 0:NT - 1])
                put(dst[1 + G * G + TX * (NT - 1):N], y[TGL + 1:TL, NT - 1])

            sp.sem_inc(sem["out_written"], START["out_written"])
            sp.wait_ge(setup_done, 1)
            for half in range(2):
                sp.dma_start(h[TGL:TGL + 1, half, NT - 1, :], cls[0:1, 0, :]).then_inc(cls_placed, 16)

            def step(i, prep, att, fin, parity, ahead=True):
                if att:
                    sp.wait_ge(sem["s_filled"], upto("s_filled", i, 0))
                    sp.wait_ge(sem["m_filled"], upto("m_filled", i, 84))
                    sp.wait_ge(sem["shift_written"], upto("shift_written", i, 16))
                    load_group(1, 1 - parity, "group_loaded_1")
                    load_shift(1, 1 - parity)
                if prep:
                    load_txt(i + 1, 1 - parity)
                    if ahead:
                        load_x(i + 2)
                if att:
                    sp.wait_ge(sem["s_filled"], upto("s_filled", i, 28))
                    load_group(2, parity, "group_loaded_2")
                    load_shift(2, parity)
                if prep:
                    write_parts(i + 1, 1 - parity)
                    sp.wait_ge(sem["s_filled"], upto("s_filled", i, 56))
                    for c in range(3):
                        sp.wait_ge(sem[f"parts_written_{c}"], upto(f"parts_written_{c}", i + 1, 16))
                    load_group(0, 1 - parity, "group_loaded_0")
                if prep:
                    sp.wait_ge(sem["flag_ready"], upto("flag_ready", i + 1, 1))
                    sp.sem_inc(sem["flag_seen"], 1)
                    with sp.If(sp.value_load(flag[0:1, 1 - parity:2 - parity]) > 0):
                        load_for_maxima(i + 1, parity)
                        send_shift(i + 1, 1 - parity)
                    with sp.Else():
                        sp.sem_inc(sem["m_loaded"], PER["m_loaded"])
                        sp.dma_start(scr_shift, t["no_shift"]).then_inc(sem["shift_written"], 16)
                        sp.dma_start(Qs[KR:KS, 1 - parity], t["no_shift"][:, 0:4]).then_inc(sem["shift_loaded_0"], 16)
                if fin:
                    store(i - 1)

            step(-1, True, False, False, 1)
            step(0, True, True, False, 0)
            with sp.Fori(0, (B - 2) // 2 - 1) as j:
                step(2 * j + 1, True, True, True, 1)
                step(2 * j + 2, True, True, True, 0)
            step(B - 3, True, True, True, 1)
            step(B - 2, True, True, True, 0, ahead=False)
            step(B - 1, False, True, True, 1)
            step(B, False, False, True, 0)
            sp.wait_ge(sem["out_written"], upto("out_written", B, 0))

        @block.tensor
        def _(pe):
            mm = nc.tensor.matmul

            def prepare(a, fill, half):
                bank, (kind, k) = ps_a, fill
                pe.wait_ge(sem["a_drained"], upto("a_drained", a, a_nth[fill] - 1))
                if kind == "conv":
                    if k == 0:
                        pe.wait_ge(sem["x_loaded"], upto("x_loaded", a, 48))
                    g = 3 if k == NT - 1 else GR
                    r0 = GR * k
                    o = bank[0:g * G, 0:D]
                    for q, (dr, dc) in enumerate(((0, 0), (0, 1), (1, 0), (1, 1))):
                        last = mm(o, xa[:, dc, G * (r0 + dr):G * (r0 + dr + g)], w_conv[:, q],
                                  start=(q == 0), stop=False)
                    for dr in range(2):
                        last = mm(o, xb[:, G * (r0 + dr):G * (r0 + dr + g)], w_conv[:, 4 + dr],
                                  start=False, stop=(dr == 1))
                    last.then_inc(sem["a_filled"], 1)
                elif kind == "xnT":
                    if k == 0:
                        pe.wait_ge(setup_done, 1)
                        pe.wait_ge(sem["xn_ready"], upto("xn_ready", a, 1))
                    hf, tiles = quads[k]
                    for n, tile in enumerate(tiles):
                        last = nc.tensor.transpose(bank[0:96, n * TS:n * TS + rows(tile)],
                                                   xn[0:rows(tile), tile, 96 * hf:96 * hf + 96],
                                                   ident[0:rows(tile), 0:rows(tile)])
                    last.then_inc(sem["a_filled"], 1)
                elif kind == "qk":
                    c, hf = divmod(k, 2)
                    for kk in range(2):
                        last = mm(bank[:, 0:HF], w_qk[:, kk, 128 * c:128 * c + 128], xnT[0:96, kk, hf * HF:hf * HF + HF],
                                  start=(kk == 0), stop=(kk == 1))
                    last.then_inc(sem["a_filled"], 1)
                elif kind == "bound":
                    pe.wait_ge(sem["bound_chain"], upto("bound_chain", a, 1))
                    for c in range(3):
                        last = mm(bank[0:1, 128 * c:128 * c + 128], top[:, c, 0:1], ident[:], start=True, stop=True,
                                  skip_group_check=True)
                    last.then_inc(sem["a_filled"], 1)
                else:
                    for n, tile in enumerate(pairs[k]):
                        for kk in range(2):
                            kp = 96 + kk
                            last = mm(bank[0:TL, n * D:n * D + D], xnT[0:kp, kk, TS * tile:TS * tile + TL],
                                      w_v[0:kp, kk], start=(kk == 0), stop=(kk == 1), skip_group_check=True)
                    last.then_inc(sem["a_filled"], 1)

            def finish(c, fill):
                bank, (kind, k) = ps_c, fill
                pe.wait_ge(sem["c_drained"], upto("c_drained", c, c_nth[fill] - 1))
                if kind == "proj":
                    if k == 0:
                        pe.wait_ge(sem["o_ready"], upto("o_ready", c, 3))
                    for n, tile in enumerate(pairs[k]):
                        for slab in range(2):
                            last = mm(bank[0:TL, n * D:n * D + D], oT[:, slab, TS * tile:TS * tile + TL],
                                      w_p[:, slab], start=(slab == 0), stop=(slab == 1), skip_group_check=True)
                elif kind == "x2T":
                    if k == 0:
                        pe.wait_ge(sem["x2_ready"], upto("x2_ready", c, 1))
                    hf, tiles = quads[k]
                    for n, tile in enumerate(tiles):
                        last = nc.tensor.transpose(bank[0:96, n * TS:n * TS + rows(tile)],
                                                   x2[0:rows(tile), tile, 96 * hf:96 * hf + 96],
                                                   ident[0:rows(tile), 0:rows(tile)])
                elif kind == "logits":
                    for tile in quads[k][1]:
                        for kk in range(2):
                            last = mm(bank[0:TL, tile * NS:tile * NS + NS], x2T[:, kk, TS * tile:TS * tile + TL],
                                      slots[:, kk], start=(kk == 0), stop=(kk == 1), skip_group_check=True)
                elif kind == "lT":
                    for n, tile in enumerate(quads[k][1]):
                        last = nc.tensor.transpose(bank[0:NS, n * TS:n * TS + rows(tile)],
                                                   disp[0:rows(tile), tile], ident[0:rows(tile), 0:rows(tile)])
                elif kind == "disp":
                    pe.wait_ge(sem["diag_ready"], upto("diag_ready", c, 1))
                    for tile in range(NT):
                        last = mm(bank[0:TL, tile * NS:tile * NS + NS], lT[:, TS * tile:TS * tile + TL], diag[:],
                                  start=True, stop=True, skip_group_check=True)
                elif kind == "cT":
                    pe.wait_ge(sem["comb_exp"], upto("comb_exp", c, 1))
                    for n, tile in enumerate(quads[k][1]):
                        last = nc.tensor.transpose(bank[0:NS, n * TS:n * TS + rows(tile)], lc[0:rows(tile), tile],
                                                   ident[0:rows(tile), 0:rows(tile)])
                elif kind == "xt":
                    for tile in range(NT):
                        m = rows(tile)
                        last = mm(bank[0:96, 0:NS], x2[0:m, tile, 96 * k:96 * k + 96], disp[0:m, tile],
                                  start=(tile == 0), stop=(tile == NT - 1))
                elif kind == "hidden":
                    for m in range(2):
                        for kk in range(2):
                            last = mm(bank[0:96, m * NS:m * NS + NS], w_down[:, kk, 96 * m:96 * m + 96], xt[:, kk],
                                      start=(kk == 0), stop=(kk == 1), skip_group_check=True)
                elif kind == "yt":
                    pe.wait_ge(sem["hidden_ready"], upto("hidden_ready", c, 1))
                    for m in range(2):
                        last = mm(bank[0:NS, 0:D], hm[:, m], w_up[:, m], start=(m == 0), stop=(m == 1))
                else:
                    for n, tile in enumerate(pairs[k]):
                        last = mm(bank[0:TL, n * D:n * D + D], cT[:, TS * tile:TS * tile + TL], yt[:],
                                  start=True, stop=True, skip_group_check=True)
                last.then_inc(sem["c_filled"], 1)

            def scores(b, unit, j, half):
                g, tile = divmod(unit, NT)
                n = 4 * unit + j
                pe.wait_ge(sem["exp_done"], upto("exp_done", b, n - 1))
                if tile == 0 and j == 0:
                    pe.wait_ge(sem[f"group_loaded_{g}"], upto(f"group_loaded_{g}", b, 192))
                    pe.wait_ge(sem[f"shift_loaded_{g}"], upto(f"shift_loaded_{g}", b, 16))
                for hf in range(2):
                    last = mm(ps_s[0:rows(tile), n % 2, hf, 0:HF],
                              Ks[:, (half + g) % 2, j, TS * tile:TS * tile + rows(tile)],
                              Qs[:, (half + g) % 2, j, hf * HF:hf * HF + HF], start=True, stop=True)
                last.then_inc(sem["s_filled"], 1)

            def weigh(b, unit, half, hf):
                g, tile = divmod(unit, NT)
                m = rows(tile)
                if hf == 0:
                    pe.wait_ge(sem["exp_done"], upto("exp_done", b, 4 * unit + 4))
                    if unit == 0:
                        pe.wait_ge(sem["a_drained"], upto("a_drained", b, a_nth["v", 3]))
                if tile == 0:
                    pe.wait_ge(sem["o_bcast"], upto("o_bcast", b, 2 * g - 1 + hf))
                for j in range(4):
                    last = mm(ps_o[32 * j:32 * j + HD + 1, hf, 0:HF], v[0:m, half, tile, 4 * g + j],
                              probs[0:m, (half + unit) % 2, j, hf * HF:hf * HF + HF],
                              start=(tile == 0), stop=(tile == NT - 1), tile_position=(0, 32 * j))
                last.then_inc(sem["pv_done"], 1)

            def maxima(a, half):
                pe.wait_ge(sem["group_loaded_0"], upto("group_loaded_0", a, 192))
                for head in range(NH):
                    g, j = divmod(head, 4)
                    if j == 0 and g:
                        pe.wait_ge(sem["m_loaded"], upto("m_loaded", a, 192 * g))
                    at = half if g == 0 else 1 - half
                    for tile in range(NT):
                        n = head * NT + tile
                        if n >= 2:
                            pe.wait_ge(sem["m_drained"], upto("m_drained", a, n - 1))
                        else:
                            pe.wait_ge(sem["exp_done"], upto("exp_done", a - 1, 84))
                        for hf in range(2):
                            lo = hf * (HF - 1)
                            last = mm(ps_s[0:TL, n % 2, hf, 0:HF], Qs[0:KR, at, j, TS * tile:TS * tile + TL],
                                      Ks[0:KR, at, j, lo:lo + HF], start=True, stop=True)
                        last.then_inc(sem["m_filled"], 1)
                for n, tiles in enumerate(((0, 1, 2, 3), (4, 5, 6))):
                    pe.wait_ge(sem["m_drained"], upto("m_drained", a, 84))
                    for q, tile in enumerate(tiles):
                        last = nc.tensor.transpose(ps_s[0:NH, 0, n, q * TS:q * TS + rows(tile)],
                                                   mx[0:rows(tile), tile], ident[0:rows(tile), 0:rows(tile)])
                    last.then_inc(sem["m_filled"], 1)

            def step(i, prep, att, fin, parity):
                for q in range(4 * UNITS):
                    unit, j = divmod(q, 4)
                    if att and unit + 1 < UNITS:
                        scores(i, unit + 1, j, parity)
                    if prep and q == 4 * (UNITS - 1):
                        pe.wait_ge(sem["flag_ready"], upto("flag_ready", i + 1, 1))
                        pe.sem_inc(sem["flag_seen"], 1)
                        with pe.If(pe.value_load(flag[0:1, 1 - parity:2 - parity]) > 0):
                            maxima(i + 1, 1 - parity)
                        with pe.Else():
                            pe.sem_inc(sem["m_filled"], PER["m_filled"])
                    if prep and unit + 1 == UNITS:
                        scores(i + 1, 0, j, 1 - parity)
                    if att and j in (1, 2):
                        weigh(i, unit, parity, j - 1)
                    if q in FILLS:
                        if FILLS[q][0] in PREPARES:
                            if prep:
                                prepare(i + 1, FILLS[q], 1 - parity)
                        elif fin:
                            finish(i - 1, FILLS[q])

            pe.wait_ge(w_conv_loaded, 16)
            step(-1, True, False, False, 1)
            step(0, True, True, False, 0)
            with pe.Fori(0, (B - 2) // 2) as j:
                step(2 * j + 1, True, True, True, 1)
                step(2 * j + 2, True, True, True, 0)
            step(B - 1, False, True, True, 1)
            step(B, False, False, True, 0)

        @block.scalar
        def _(act):
            def exps(b, unit, j, half):
                g, tile = divmod(unit, NT)
                m = rows(tile)
                n = 4 * unit + j
                act.wait_ge(sem["s_filled"], upto("s_filled", b, n + 1))
                if j == 0:
                    act.wait_ge(sem["pv_done"], upto("pv_done", b, 2 * (unit - 1)))
                nc.scalar.activation(probs[0:m, (half + unit) % 2, j].rearrange("p (a n) -> p a n", a=2),
                                     ps_s[0:m, n % 2, :, 0:HF], ACT.Exp).then_inc(sem["exp_done"], 1)

            def guess(b, g, part):
                if part == 0:
                    act.wait_ge(sem["o_bcast"], upto("o_bcast", b, 2 * g + 2))
                    nc.scalar.activation(rec[:], den[:], ACT.Ln).then_inc(sem["o_guess"], 1)
                else:
                    act.wait_ge(sem["o_guess"], upto("o_guess", b, 2 * g + 1))
                    nc.scalar.activation(rec[:], rec[:], ACT.Exp, scale=-1.0).then_inc(sem["o_guess"], 1)

            def copy_qk(a, k, half):
                c, hf = divmod(k, 2)
                act.wait_ge(sem["a_filled"], upto("a_filled", a, a_nth["qk", k]))
                if hf == 0:
                    act.wait_ge(sem["r_ready"], upto("r_ready", a, 2 * (c - 1)))
                nc.scalar.activation(f[:, (half + c) % 2, hf * HF:hf * HF + HF], ps_a[:, 0:HF], ACT.Identity,
                                     bias=b_qk[:, c:c + 1])\
                    .then_inc(sem["a_drained"], 1)

            GUESS = {0: (29, 32), 1: (57, 60), NG - 1: (0, 1)}

            def copy_x2T(c, k):
                hf, tiles = quads[k]
                c0 = TS * tiles[0]
                c1 = TS * tiles[-1] + rows(tiles[-1])
                act.wait_ge(sem["c_filled"], upto("c_filled", c, c_nth["x2T", k]))
                nc.scalar.activation(x2T[:, hf, c0:c1], ps_c[0:96, 0:c1 - c0], ACT.Identity)\
                    .then_inc(sem["c_drained"], 1)

            def step(i, prep, att, fin, parity):
                for q in range(4 * UNITS):
                    unit, j = divmod(q, 4)
                    if att and unit + 1 < UNITS:
                        exps(i, unit + 1, j, parity)
                    if prep and unit + 1 == UNITS:
                        exps(i + 1, 0, j, 1 - parity)
                    for g in GUESS:
                        if (att if g < NG - 1 else fin) and q in GUESS[g]:
                            guess(i if g < NG - 1 else i - 1, g, GUESS[g].index(q))
                    if prep and FILLS.get(q, ("", 0))[0] == "qk":
                        copy_qk(i + 1, FILLS[q][1], 1 - parity)
                    if fin and FILLS.get(q, ("", 0))[0] == "x2T":
                        copy_x2T(i - 1, FILLS[q][1])
                    if fin and q == AT["lT", 1] + 2:
                        act.wait_ge(sem["c_chain"], upto("c_chain", i - 1, 2))
                        nc.scalar.activation(lT[:, 0:N], lT[:, 0:N], ACT.Exp, bias=nmax[:], accum_out=dsum[:])\
                            .then_inc(sem["disp_exp"], 1)
                    if fin and q == AT["lT", 1] + 1:
                        act.wait_ge(sem["combine_ready"], upto("combine_ready", i - 1, 1))
                        nc.scalar.activation(lc[:], lc[:], ACT.Exp).then_inc(sem["comb_exp"], 1)

            act.preload_act_table_set("natural_log_exp_and_others")
            act.wait_ge(setup_done, 1)
            step(-1, True, False, False, 1)
            step(0, True, True, False, 0)
            with act.Fori(0, (B - 2) // 2) as j:
                step(2 * j + 1, True, True, True, 1)
                step(2 * j + 2, True, True, True, 0)
            step(B - 1, False, True, True, 1)
            step(B, False, False, True, 0)

        @block.vector
        def _(dve):
            V = nc.vector
            made = [0]

            def link(ins):
                made[0] += 1
                ins.then_inc(setup_dve, 1)
                dve.wait_ge(setup_dve, made[0])

            dve.sem_inc(sem["c_drained"], START["c_drained"])
            V.memset(h[:].rearrange("p a t d -> p (a t d)"), 0.0)
            V.memset(xnT[0:96, :, N:NP], 0.0)
            V.memset(xnT[96:97], 1.0)
            V.memset(x2T[:, :, N:NP], 0.0)
            V.memset(Ks[KR:KS].rearrange("p a t d -> p (a t d)"), 1.0)
            V.memset(v[:, :, :, :, HD:HD + 1].rearrange("p a t g d -> p (a t g) d"), 1.0)
            V.memset(ps_o[:], 0.0)
            V.memset(neg[:], 0.0)
            V.memset(ve2[:, :, NT:8], 1.0)
            for n, value in enumerate((-0.5, 0.5, -1.0, LN_EPS, L2_EPS, float(D), 0.0)):
                last = V.memset(const[:, n], value)
            link(last)
            dve.wait_ge(params_loaded, 17 * 16)
            V.tensor_tensor(pos[:], pos[:], tokb[:].unsqueeze(1).to_broadcast([TG, NT, D]), ALU.add)
            V.tensor_tensor(cls[:, 0], cls[:, 0], cls[:, 1], ALU.add)
            V.tensor_scalar(w_qk[:, :, 0:D], w_qk[:, :, 0:D], HD ** -0.5, None, ALU.mult)
            V.tensor_scalar(b_qk[:, 0:1], b_qk[:, 0:1], HD ** -0.5, None, ALU.mult)
            V.tensor_scalar(b_qk[0:D - 128, 1:2], b_qk[0:D - 128, 1:2], HD ** -0.5, None, ALU.mult)
            link(V.tensor_tensor(sq[:], slots[:], slots[:], ALU.mult))
            link(V.tensor_reduce(nrm[:], sq[:].rearrange("p k (e s) -> p k s e", e=NEXP), axis=AX.X, op=ALU.add))
            dve.wait_ge(setup_pool, 1)
            link(V.tensor_scalar(nrm[:], nrm[:], L2_EPS, None, ALU.add))
            link(V.reciprocal(nrm[:], nrm[:]))
            link(V.tensor_scalar(nrm[:], nrm[:], scale_c[:], None, ALU.mult))
            for kk in range(2):
                last = V.tensor_tensor(slots[:, kk].rearrange("p (e s) -> p e s", e=NEXP),
                                       slots[:, kk].rearrange("p (e s) -> p e s", e=NEXP),
                                       nrm[:, kk].unsqueeze(1).to_broadcast([96, NEXP, SLOTS]), ALU.mult)
            last.then_inc(setup_done, 1)
            dve.wait_ge(cls_placed, 32)

            def prepare(a, fill, half):
                kind, k = fill
                if kind != "qk":
                    dve.wait_ge(sem["a_filled"], upto("a_filled", a, a_nth[fill]))
                if kind == "conv":
                    m = TGL if k == NT - 1 else TG
                    dve.wait_ge(sem["c_drained"], upto("c_drained", a - 2, c_nth["proj", k // 2]))
                    V.tensor_tensor(h[0:m, half, k], ps_a[0:m, 0:D], pos[0:m, k], ALU.add)\
                        .then_inc(sem["a_drained"], 1)
                elif kind == "xnT":
                    hf, tiles = quads[k]
                    c0 = TS * tiles[0]
                    c1 = TS * tiles[-1] + rows(tiles[-1])
                    V.tensor_copy(xnT[0:96, hf, c0:c1], ps_a[0:96, 0:c1 - c0]).then_inc(sem["a_drained"], 1)
                elif kind == "qk":
                    c, hf = divmod(k, 2)
                    cols = slice(hf * HF, hf * HF + HF)
                    buf = (half + c) % 2
                    dve.wait_ge(sem["a_drained"], upto("a_drained", a, a_nth[fill]))
                    before = (c + 1) % 3
                    dve.wait_ge(sem[f"parts_written_{before}"], upto(f"parts_written_{before}", a, 16 if c == 2 else 0))
                    V.tensor_copy(parts[:, buf, 0, cols], f[:, buf, cols]).then_inc(sem["hi_ready"], 1)
                    V.tensor_reduce(top[:, c, hf:hf + 1], f[:, buf, cols], axis=AX.X, op=ALU.max,
                                    apply_absolute_value=True)
                    dve.wait_ge(sem["hi_ready"], upto("hi_ready", a, k + 1))
                    V.tensor_tensor(r[:, buf, cols], f[:, buf, cols], parts[:, buf, 0, cols], ALU.subtract)\
                        .then_inc(sem["r_ready"], 1)
                elif kind == "bound":
                    V.tensor_copy(bound[:], ps_a[0:1, 0:2 * D]).then_inc(sem["a_drained"], 1)
                    dve.wait_ge(sem["a_drained"], upto("a_drained", a, a_nth[fill]))
                    V.tensor_tensor(bound[:, 0:D], bound[:, 0:D], bound[:, D:2 * D], ALU.mult)\
                        .then_inc(sem["bound_chain"], 1)
                    dve.wait_ge(sem["bound_chain"], upto("bound_chain", a, 2))
                    V.tensor_reduce(head_bound[:], bound[:, 0:D].rearrange("p (h d) -> p h d", d=HD), axis=AX.X,
                                    op=ALU.add).then_inc(sem["bound_chain"], 1)
                    dve.wait_ge(sem["bound_chain"], upto("bound_chain", a, 3))
                    V.tensor_reduce(most[:], head_bound[:], axis=AX.X, op=ALU.max).then_inc(sem["bound_chain"], 1)
                    dve.wait_ge(sem["bound_chain"], upto("bound_chain", a, 4))
                    dve.wait_ge(sem["flag_seen"], upto("flag_seen", a - 1, 0))
                    V.tensor_scalar(flag[0:1, half:half + 1], most[:], LIMIT, None, ALU.is_gt)\
                        .then_inc(sem["flag_ready"], 1)
                else:
                    n, t0 = len(pairs[k]), pairs[k][0]
                    V.tensor_copy(v[:, half, t0:t0 + n, :, 0:HD],
                                  ps_a[0:TL, 0:n * D].rearrange("p (t g d) -> p t g d", g=NH, d=HD))\
                        .then_inc(sem["a_drained"], 1)

            def bounds(a):
                dve.wait_ge(sem["r_ready"], upto("r_ready", a, 6))
                V.tensor_tensor(top[:, :, 0], top[:, :, 0], top[:, :, 1], ALU.max).then_inc(sem["bound_chain"], 1)

            def carry(n):
                V.memset(held[:, n:n + 1], 0.0)

            def stats1(a, tile, half):
                dve.wait_ge(sem["a_drained"], upto("a_drained", a, a_nth["conv", tile]))
                if tile == 0:
                    dve.wait_ge(sem["txt_loaded"], upto("txt_loaded", a, 32))
                    carry(0)
                V.bn_stats(st[:, tile], h[:, half, tile]).then_inc(sem["stats_done"], 1)

            def stats2(c, k):
                dve.wait_ge(sem["c_drained"], upto("c_drained", c, c_nth["proj", k]))
                for tile in pairs[k]:
                    last = V.bn_stats(st2[:, tile], h2[:, tile])
                last.then_inc(sem["stats2_done"], 1)

            def combine(into, agg, done, chain, image, n):
                dve.wait_ge(sem[done], upto(done, image, PER[done]))
                carry(n)
                for tile in range(NT):
                    last = V.bn_aggr(agg[:, tile], into[:, tile])
                last.then_inc(sem[chain], 1)

            def factor2(c):
                dve.wait_ge(sem["ln2_pool"], upto("ln2_pool", c, 3))
                V.tensor_tensor(sc2[:, 0, 0:NT], pow2[:, 0, 0:NT], pow2[:, 1, 0:NT], ALU.mult)\
                    .then_inc(sem["ln2_chain"], 1)
                dve.wait_ge(sem["ln2_chain"], upto("ln2_chain", c, 2))
                V.tensor_scalar(sc2[:, 0, 0:NT], sc2[:, 0, 0:NT], L2_EPS, None, ALU.add).then_inc(sem["ln2_chain"], 1)
                dve.wait_ge(sem["ln2_chain"], upto("ln2_chain", c, 3))
                V.reciprocal(sc2[:, 0, 0:NT], sc2[:, 0, 0:NT]).then_inc(sem["ln2_chain"], 1)
                dve.wait_ge(sem["ln2_chain"], upto("ln2_chain", c, 4))
                V.tensor_tensor(sc2[:, 1, 0:NT], sc2[:, 0, 0:NT], pow2[:, 0, 0:NT], ALU.mult)\
                    .then_inc(sem["ln2_chain"], 1)
                dve.wait_ge(sem["ln2_chain"], upto("ln2_chain", c, 5))

            def normalise(dst, src, agg, factor, ready):
                for tile in range(NT):
                    last = V.tensor_scalar(dst[:, tile], src[:, tile], agg[:, tile, 0:1], factor[:, tile:tile + 1],
                                           ALU.subtract, ALU.mult)
                last.then_inc(sem[ready], 1)

            def maxima(a):
                for n in range(TILES):
                    head, tile = divmod(n, NT)
                    dve.wait_ge(sem["m_filled"], upto("m_filled", a, n + 1))
                    V.tensor_reduce(mx[:, tile, head:head + 1], ps_s[0:TL, n % 2, :, 0:HF], axis=AX.XY, op=ALU.max)\
                        .then_inc(sem["m_drained"], 1)
                dve.wait_ge(sem["shift_written"], upto("shift_written", a, 0))
                dve.wait_ge(sem["m_filled"], upto("m_filled", a, 86))
                V.tensor_scalar(neg[:, 0:4 * TS], ps_s[0:NH, 0, 0, 0:4 * TS], -1.0, None, ALU.mult)
                V.tensor_scalar(neg[:, 4 * TS:N], ps_s[0:NH, 0, 1, 0:N - 4 * TS], -1.0, None, ALU.mult)\
                    .then_inc(sem["m_chain"], 1)
                dve.wait_ge(sem["m_chain"], upto("m_chain", a, 1))
                V.tensor_copy(shift[:, 0], neg[:]).then_inc(sem["m_chain"], 1)
                dve.wait_ge(sem["m_chain"], upto("m_chain", a, 2))
                V.tensor_tensor(shift[:, 1], neg[:], shift[:, 0], ALU.subtract).then_inc(sem["shift_ready"], 1)

            def collect(b, g, hf):
                cols = slice(hf * HF, hf * HF + HF)
                dve.wait_ge(sem["pv_done"], upto("pv_done", b, 2 * NT * (g + 1) - 1 + hf))
                dve.wait_ge(sem["c_filled"], upto("c_filled", b - 1, c_nth["proj", 3]))
                if g < NG - 1:
                    V.tensor_copy(oT[:, g, cols], ps_o[:, hf, 0:HF]).then_inc(sem["o_copied"], 1)
                else:
                    carry(3 + hf)
                    V.stream_shuffle(oT[:, g, cols], ps_o[:, hf, 0:HF], [0] * HD + list(range(HD)))\
                        .then_inc(sem["o_copied"], 1)
                if hf == 0:
                    dve.wait_ge(sem["o_ready"], upto("o_ready", b, g))
                    carry(2)
                V.stream_shuffle(den[:, cols], ps_o[:, hf, 0:HF], [HD] * 32).then_inc(sem["o_bcast"], 1)

            def divide(b, g, part):
                if part == 0:
                    dve.wait_ge(sem["o_guess"], upto("o_guess", b, 2 * g + 2))
                    V.tensor_tensor(den[:], den[:], rec[:], ALU.mult).then_inc(sem["o_chain"], 1)
                elif part == 1:
                    dve.wait_ge(sem["o_chain"], upto("o_chain", b, 2 * g + 1))
                    V.scalar_tensor_tensor(den[:], den[:], 2.0, rec[:], ALU.subtract, ALU.mult)\
                        .then_inc(sem["o_chain"], 1)
                elif part == 2:
                    dve.wait_ge(sem["o_chain"], upto("o_chain", b, 2 * g + 2))
                    factor = (-1.0, minus_first[:], minus_last[:])[g]
                    V.scalar_tensor_tensor(oT[:, g], oT[:, g], factor, den[:], ALU.mult, ALU.mult)\
                        .then_inc(*((sem["o_ready"], 1) if g < NG - 1 else (sem["o_chain"], 1)))
                else:
                    dve.wait_ge(sem["o_chain"], upto("o_chain", b, 2 * g + 3))
                    dve.wait_ge(sem["o_ready"], upto("o_ready", b, g))
                    V.tensor_tensor(oT[:, 1], oT[:, 1], oT[:, 2], ALU.add).then_inc(sem["o_ready"], 1)

            step_count = [0]

            def chain(ins, c, behind=0):
                step_count[0] += 1
                ins.then_inc(sem["c_chain"], 1)
                dve.wait_ge(sem["c_chain"], upto("c_chain", c, step_count[0] - behind))

            def finish(c, fill, half):
                kind, k = fill
                dve.wait_ge(sem["c_filled"], upto("c_filled", c, c_nth[fill]))
                drained = lambda ins: ins.then_inc(sem["c_drained"], 1)
                if kind == "proj":
                    n, t0 = len(pairs[k]), pairs[k][0]
                    drained(V.tensor_tensor(h2[:, t0:t0 + n], ps_c[0:TL, 0:n * D].rearrange("p (t d) -> p t d", d=D),
                                            h[:, half, t0:t0 + n], ALU.add))
                elif kind in ("lT", "cT"):
                    tiles = quads[k][1]
                    c0 = TS * tiles[0]
                    c1 = TS * tiles[-1] + rows(tiles[-1])
                    drained(V.tensor_copy((lT if kind == "lT" else cT)[:, c0:c1], ps_c[0:NS, 0:c1 - c0]))
                elif kind == "logits":
                    tiles = quads[k][1]
                    c0, c1 = tiles[0], tiles[-1] + 1
                    drained(V.tensor_copy(disp[:, c0:c1].rearrange("p t s -> p (t s)"),
                                          ps_c[0:TL, NS * c0:NS * c1]))
                elif kind == "disp":
                    drained(V.tensor_copy(disp[:].rearrange("p t s -> p (t s)"), ps_c[0:TL, 0:NT * NS]))
                elif kind == "xt":
                    drained(V.tensor_copy(xt[:, k], ps_c[0:96, 0:NS]))
                elif kind == "hidden":
                    drained(V.tensor_tensor(u[:], ps_c[0:96, 0:2 * NS].rearrange("p (a s) -> p a s", s=NS),
                                            b_down[:].unsqueeze(2).to_broadcast([96, 2, NS]), ALU.add))
                    dve.wait_ge(sem["c_drained"], upto("c_drained", c, c_nth[fill]))
                elif kind == "yt":
                    drained(V.tensor_tensor(yt[:], ps_c[0:NS, 0:D], b_up[:], ALU.add))
                else:
                    if k == 0:
                        dve.wait_ge(sem["out_written"], upto("out_written", c, 0))
                    for n, tile in enumerate(pairs[k]):
                        last = V.scalar_tensor_tensor(y[:, tile], ps_c[0:TL, n * D:n * D + D], crec[:, tile:tile + 1],
                                                      h2[:, tile], ALU.mult, ALU.add)
                    drained(last)

            def less_slots_max(c):
                dve.wait_ge(sem["c_drained"], upto("c_drained", c, c_nth["logits", 0]))
                chain(V.tensor_reduce(cmax[:], disp[:], axis=AX.X, op=ALU.max), c)
                V.tensor_tensor(lc[:], disp[:], cmax[:].unsqueeze(2).to_broadcast([TL, NT, NS]), ALU.subtract)\
                    .then_inc(sem["combine_ready"], 1)

            def tokens_max(c):
                dve.wait_ge(sem["c_drained"], upto("c_drained", c, c_nth["lT", 1]))
                chain(V.tensor_reduce(nmax[:], lT[:, 0:N], axis=AX.X, op=ALU.max, negate=True), c)

            def weights(c):
                dve.wait_ge(sem["disp_exp"], upto("disp_exp", c, 1))
                chain(V.reciprocal(drec[:], dsum[:]), c)
                V.tensor_scalar(diag[:], ident[0:NS, 0:NS], drec[:], None, ALU.mult).then_inc(sem["diag_ready"], 1)
                dve.wait_ge(sem["comb_exp"], upto("comb_exp", c, 1))
                chain(V.tensor_reduce(csum[:], lc[:], axis=AX.X, op=ALU.add), c)
                chain(V.reciprocal(crec[:], csum[:]), c)

            def gelu(c, part):
                if part == 0:
                    chain(V.tensor_scalar(uc[:], u[:], 0.5 ** 0.5, ERF_MAX, ALU.mult, ALU.min), c)
                    chain(V.tensor_scalar(uc[:], uc[:], -ERF_MAX, None, ALU.max), c)
                    chain(V.tensor_tensor(u2[:], uc[:], uc[:], ALU.mult), c)
                elif part == 1:
                    chain(V.tensor_scalar(pd[:], u2[:], ERF_DEN[0], None, ALU.mult), c, 1)
                    chain(V.tensor_scalar(pn[:], u2[:], ERF_NUM[0], None, ALU.mult), c, 1)
                    for coef_d, coef_n in zip(ERF_DEN[1:], ERF_NUM[1:]):
                        chain(V.scalar_tensor_tensor(pd[:], pd[:], coef_d, u2[:], ALU.add, ALU.mult), c, 1)
                        chain(V.scalar_tensor_tensor(pn[:], pn[:], coef_n, (uc if coef_n == ERF_NUM[-1] else u2)[:],
                                                     ALU.add, ALU.mult), c, 1)
                    chain(V.scalar_tensor_tensor(pd[:], pd[:], ERF_DEN[-2], u2[:], ALU.add, ALU.mult), c)
                else:
                    chain(V.tensor_scalar(pd[:], pd[:], ERF_DEN[-1], None, ALU.add), c)
                    chain(V.reciprocal(pd[:], pd[:]), c)
                    chain(V.tensor_tensor(pn[:], pn[:], pd[:], ALU.mult), c)
                    chain(V.scalar_tensor_tensor(pn[:], pn[:], 1.0, u[:], ALU.add, ALU.mult), c)
                    V.scalar_tensor_tensor(hm[:], pn[:], 0.5, mask[:], ALU.mult, ALU.mult)\
                        .then_inc(sem["hidden_ready"], 1)

            DIVIDE = {0: (35, 37, 40), 1: (62, 66, 69), NG - 1: (2, 3, 4, 5)}
            COMBINE1, NORM1 = AT["conv", NT - 1], AT["conv", NT - 1] + 3
            COMBINE2, NORM2 = AT["proj", 3], AT["proj", 3] + 3
            WEIGHTS, GELU, BOUNDS = AT["lT", 1] + 5, (56, 57, 58), 58

            def step(i, prep, att, fin, parity):
                step_count[0] = 0
                for q in range(4 * UNITS):
                    unit, j = divmod(q, 4)
                    if prep and q == 4 * (UNITS - 1):
                        dve.wait_ge(sem["flag_ready"], upto("flag_ready", i + 1, 1))
                        dve.sem_inc(sem["flag_seen"], 1)
                        with dve.If(dve.value_load(flag[0:1, 1 - parity:2 - parity]) > 0):
                            maxima(i + 1)
                        with dve.Else():
                            dve.sem_inc(sem["m_drained"], PER["m_drained"])
                            dve.sem_inc(sem["m_chain"], PER["m_chain"])
                            dve.sem_inc(sem["shift_ready"], PER["shift_ready"])
                    if att and unit % NT == NT - 1 and j in (1, 2):
                        collect(i, unit // NT, j - 1)
                    if q in FILLS:
                        if FILLS[q][0] in PREPARES:
                            if prep and FILLS[q] != ("conv", 0):
                                prepare(i + 1, FILLS[q], 1 - parity)
                        elif fin and FILLS[q][0] != "x2T":
                            finish(i - 1, FILLS[q], 1 - parity)
                            if FILLS[q] == ("lT", 0):
                                less_slots_max(i - 1)
                            if FILLS[q] == ("lT", 1):
                                tokens_max(i - 1)
                    if prep and q == AT["proj", 0]:
                        prepare(i + 1, ("conv", 0), 1 - parity)
                    if prep and q >= AT["proj", 3]:
                        for tile in range(NT):
                            if q == max(AT["conv", tile], AT["proj", 3] + 1 + tile // 2):
                                stats1(i + 1, tile, 1 - parity)
                    if fin and FILLS.get(q, ("", 0))[0] == "proj":
                        stats2(i - 1, FILLS[q][1])
                    if fin and q == COMBINE2:
                        combine(st2, mv2, "stats2_done", "ln2_chain", i - 1, 1)
                    if fin and q == NORM2:
                        factor2(i - 1)
                        normalise(x2, h2, mv2, sc2[:, 1], "x2_ready")
                    if prep and q == COMBINE1:
                        combine(st, mv, "stats_done", "a_chain", i + 1, 0)
                    if prep and q == NORM1:
                        dve.wait_ge(sem["ln1_pool"], upto("ln1_pool", i + 1, 2))
                        normalise(xn, h[:, 1 - parity], mv, rstd, "xn_ready")
                    for g in DIVIDE:
                        if (att if g < NG - 1 else fin) and q in DIVIDE[g]:
                            divide(i if g < NG - 1 else i - 1, g, DIVIDE[g].index(q))
                    if fin and q == WEIGHTS:
                        weights(i - 1)
                    if fin and q in GELU:
                        gelu(i - 1, GELU.index(q))
                    if prep and q == BOUNDS:
                        bounds(i + 1)
                if fin:
                    assert step_count[0] == PER["c_chain"], step_count

            step(-1, True, False, False, 1)
            step(0, True, True, False, 0)
            with dve.Fori(0, (B - 2) // 2) as j:
                step(2 * j + 1, True, True, True, 1)
                step(2 * j + 2, True, True, True, 0)
            step(B - 1, False, True, True, 1)
            step(B, False, False, True, 0)

        @block.gpsimd
        def _(pool):
            G_ = nc.gpsimd
            pool.wait_ge(setup_dve, 3)
            G_.tensor_tensor(nrm[:].rearrange("p a s -> p (a s)"), nrm[:].rearrange("p a s -> p (a s)"),
                             const[0:96, 1, 0:2 * SLOTS], ALU.pow).then_inc(setup_pool, 1)

            def layernorm1(a):
                pool.wait_ge(sem["a_chain"], upto("a_chain", a, 1))
                G_.tensor_tensor(ve[:, 0:NT], mv[:, :, 1], const[0:TL, 3, 0:NT], ALU.add).then_inc(sem["ln1_pool"], 1)
                pool.wait_ge(sem["ln1_pool"], upto("ln1_pool", a, 1))
                G_.tensor_tensor(rstd[:, 0:NT], ve[:, 0:NT], const[0:TL, 0, 0:NT], ALU.pow).then_inc(sem["ln1_pool"], 1)

            def layernorm2(c):
                pool.wait_ge(sem["ln2_chain"], upto("ln2_chain", c, 1))
                G_.tensor_tensor(ve2[:, 0, 0:NT], mv2[:, :, 1], const[0:TL, 3, 0:NT], ALU.add)\
                    .then_inc(sem["ln2_pool"], 1)
                G_.tensor_tensor(ve2[:, 1, 0:NT], mv2[:, :, 1], const[0:TL, 5, 0:NT], ALU.mult)\
                    .then_inc(sem["ln2_pool"], 1)
                pool.wait_ge(sem["ln2_pool"], upto("ln2_pool", c, 2))
                G_.tensor_tensor(pow2[:], ve2[:], const[0:TL, 0:2], ALU.pow).then_inc(sem["ln2_pool"], 1)

            def split(a, c, half):
                pool.wait_ge(sem["r_ready"], upto("r_ready", a, 2 * c + 2))
                buf = (half + c) % 2
                G_.tensor_tensor(parts[:, buf, 1], r[:, buf], const[:, 6, 0:1].to_broadcast([128, NP]), ALU.add)\
                    .then_inc(sem["mid_ready"], 1)
                pool.wait_ge(sem["mid_ready"], upto("mid_ready", a, c + 1))
                G_.tensor_tensor(parts[:, buf, 2], r[:, buf], parts[:, buf, 1], ALU.subtract)\
                    .then_inc(sem["parts_ready"], 1)

            def step(i, prep, att, fin, parity):
                if fin:
                    layernorm2(i - 1)
                if prep:
                    layernorm1(i + 1)
                    for c in range(3):
                        split(i + 1, c, 1 - parity)

            step(-1, True, False, False, 1)
            step(0, True, True, False, 0)
            with pool.Fori(0, (B - 2) // 2) as j:
                step(2 * j + 1, True, True, True, 1)
                step(2 * j + 2, True, True, True, 0)
            step(B - 1, False, True, True, 1)
            step(B, False, False, True, 0)


def kernel(**inputs):
    import numpy as np
    import concourse.bacc as bacc
    from concourse.bass_utils import run_bass_kernel_spmd

    inp = {k: np.asarray(v) for k, v in inputs.items()}
    f32, bf16 = np.float32, mybir.dt.np(BF16)
    B = inp["x"].shape[0]
    blocks = inp["x"].reshape(B, C, BG, S, BG, S).transpose(0, 1, 3, 5, 2, 4).reshape(B, C * S * S, BG, BG)
    x = np.stack([blocks[..., :G], blocks[..., 1:]], axis=1).reshape(B, 2, C * S * S, BG * G)
    w = inp["L0_tok_w"].reshape(D, C, 2, S, 2, S).transpose(2, 4, 1, 3, 5, 0).reshape(2, 2, C * S * S, D)
    w_conv = np.stack([w[0, 0, :128], w[0, 1, :128], w[1, 0, :128], w[1, 1, :128],
                       np.concatenate([w[0, 0, 128:], w[0, 1, 128:]]),
                       np.concatenate([w[1, 0, 128:], w[1, 1, 128:]])], axis=1)
    qkv = inp["L0_attn_qkv_w"].T.reshape(2, 96, 3 * D).transpose(1, 0, 2)
    qkv_b = inp["L0_attn_qkv_b"]
    w_v = np.zeros((97, 2, D), f32)
    w_v[:96] = qkv[:, :, 2 * D:]
    w_v[96, 1] = qkv_b[2 * D:]
    w_p = np.zeros((2, 4, 32, D), f32)
    of_groups = inp["L0_attn_proj_w"].T.reshape(NG, 4, HD, D)
    w_p[:, :, :HD] = of_groups[:2]
    w_p[1, :, HD:] = of_groups[2]
    w_p[0, 0, HD] = inp["L0_attn_proj_b"]
    position = inp["L0_tok_pos_embedding"][0]
    pos = np.zeros((TG, NT, D), f32)
    pos[:, :NT - 1] = position[1:1 + TG * (NT - 1)].reshape(NT - 1, TG, D).transpose(1, 0, 2)
    pos[:TGL, NT - 1] = position[1 + TG * (NT - 1):]
    halves = lambda a: a.reshape(2, 96, -1).transpose(1, 0, 2)
    expert = np.arange(NEXP * HID) // HID
    arrays = {
        "x": x, "txt": inp["txt"], "w_conv": w_conv,
        "w_qk": qkv[:, :, :2 * D], "b_qk": qkv_b[:2 * D].reshape(3, 128).T, "w_v": w_v,
        "w_p": w_p.reshape(2, 128, D).transpose(1, 0, 2), "pos": pos, "tok_b": inp["L0_tok_b"],
        "cls": np.concatenate([inp["L0_tok_cls_token"].reshape(1, 1, D), position[:1][None]], axis=1),
        "slots": halves(inp["L0_ffn_slot_params"].reshape(D, NS)),
        "slot_scale": inp["L0_ffn_scale"].reshape(1),
        "w_down": halves(inp["L0_ffn_W_down"].transpose(1, 0, 2).reshape(D, D)),
        "b_down": inp["L0_ffn_b_down"].reshape(2, 96).T,
        "w_up": halves(inp["L0_ffn_W_up"].reshape(D, D)),
        "b_up": np.repeat(inp["L0_ffn_b_up"], SLOTS, axis=0),
        "no_shift": np.zeros((2, NH, NP), bf16),
        "minus_first": -np.tile(np.repeat([1.0, 0.0], HD), 4)[:, None].astype(f32),
        "minus_last": -np.tile(np.repeat([0.0, 1.0], HD), 4)[:, None].astype(f32),
        "ident": np.eye(128, dtype=f32),
        "expert_mask": halves((expert[:, None] == np.arange(NS)[None] // SLOTS).astype(f32)),
    }
    arrays = {f"in_{k}": np.ascontiguousarray(v) for k, v in arrays.items()}
    nc = bacc.Bacc("TRN2", target_bir_lowering=False, num_devices=1)
    nc.disable_value_cache = True
    t = {k[3:]: nc.dram_tensor(k, v.shape, mybir.dt.from_np(v.dtype), kind="ExternalInput").ap()
         for k, v in arrays.items()}
    scr_parts = nc.dram_tensor("scr_parts", [2 * D, 3, NP], BF16, kind="Internal").ap()
    scr_shift = nc.dram_tensor("scr_shift", [2, NH, NP], BF16, kind="Internal").ap()
    out = nc.dram_tensor("out", [B, N, D], F32, kind="ExternalOutput").ap()
    early_fusion(nc, B, t, scr_parts, scr_shift, out)
    got = run_bass_kernel_spmd(nc, [arrays], core_ids=[0])
    return got.results[0]["out"]
```
